# Optimizing a Trainium2 kernel written in Bass

```python
import numpy as np
import jax
import jax.numpy as jnp

def _softmax(x, axis=-1):
    return jax.nn.softmax(x, axis=axis)

def _gelu(x):
    return jax.nn.gelu(x, approximate=True)

def _silu(x):
    return jax.nn.silu(x)

def _sigmoid(x):
    return jax.nn.sigmoid(x)

def _layernorm(x, axis=-1, eps=1e-05):
    m = jnp.mean(x, axis=axis, keepdims=True)
    v = jnp.var(x, axis=axis, keepdims=True)
    return (x - m) / jnp.sqrt(v + eps)

def _scatter_add(tgt, idx, src, axis=0):
    return tgt.at[idx].add(src)

def _segment_sum(src, seg, n):
    return jax.ops.segment_sum(src, seg, n)
kernel_name = 'mk_hybrid_d1_jaxref_r8_5093e1'

def setup_inputs(seed: int=0):
    np.random.seed(seed)
    _w = jnp.asarray

    def _L0_attn_a_setup():
        import jax, jax.numpy as jnp
        import numpy as np
        D_MODEL, D_STATE, EXPAND = (128, 16, 2)
        D_INNER = D_MODEL * EXPAND
        DT_RANK = int(np.ceil(D_MODEL / 16))
        BATCH, SEQ = (2, 256)

        def _ssm_scan(xs, A, Bs, Cs, delta):
            batch, _, d_inner = xs.shape
            n = A.shape[1]

            def step(h, inp):
                x_t, d_t, B_t, C_t = inp
                dA = jnp.exp(d_t[:, :, None] * A)
                h = dA * h + (d_t * x_t)[:, :, None] * B_t[:, None, :]
                y = jnp.einsum('bdn,bn->bd', h, C_t)
                return (h, y)
            h0 = jnp.zeros((batch, d_inner, n), jnp.float32)
            inps = (xs.transpose(1, 0, 2), delta.transpose(1, 0, 2), Bs.transpose(1, 0, 2), Cs.transpose(1, 0, 2))
            _, ys = jax.lax.scan(step, h0, inps)
            return ys.transpose(1, 0, 2)

        def _reference_tuple_inner(x, Win, bin, Wx, bx, Wdt, bdt, A_log, Dp, Wout, bout):
            xz = x @ Win + bin
            xs, z = jnp.split(xz, 2, axis=-1)
            xs = jax.nn.silu(xs)
            xp = xs @ Wx + bx
            dp = xp[..., :DT_RANK]
            Bs = xp[..., DT_RANK:DT_RANK + D_STATE]
            Cs = xp[..., DT_RANK + D_STATE:]
            delta = jax.nn.softplus(dp @ Wdt + bdt)
            A = -jnp.exp(A_log.astype(jnp.float32))
            hidden = _ssm_scan(xs, A, Bs, Cs, delta)
            y = (hidden + xs * Dp) * jax.nn.silu(z)
            out = y @ Wout + bout
            return (out, hidden)
        key = jax.random.key(seed)
        ks = jax.random.split(key, 12)
        s_in = 1.0 / np.sqrt(D_MODEL)
        s_x = 1.0 / np.sqrt(D_INNER)
        s_dt = 1.0 / np.sqrt(DT_RANK)
        return {'x': jax.random.normal(ks[0], (BATCH, SEQ, D_MODEL), jnp.float32), 'Win': jax.random.uniform(ks[1], (D_MODEL, 2 * D_INNER), jnp.float32, -s_in, s_in), 'bin': jax.random.uniform(ks[2], (2 * D_INNER,), jnp.float32, -s_in, s_in), 'Wx': jax.random.uniform(ks[3], (D_INNER, DT_RANK + 2 * D_STATE), jnp.float32, -s_x, s_x), 'bx': jax.random.uniform(ks[4], (DT_RANK + 2 * D_STATE,), jnp.float32, -s_x, s_x), 'Wdt': jax.random.uniform(ks[5], (DT_RANK, D_INNER), jnp.float32, -s_dt, s_dt), 'bdt': jax.random.uniform(ks[6], (D_INNER,), jnp.float32, -s_dt, s_dt), 'A_log': jax.random.normal(ks[7], (D_INNER, D_STATE), jnp.float32), 'Dp': jax.random.normal(ks[8], (D_INNER,), jnp.float32), 'Wout': jax.random.uniform(ks[9], (D_INNER, D_MODEL), jnp.float32, -s_x, s_x), 'bout': jax.random.uniform(ks[10], (D_MODEL,), jnp.float32, -s_x, s_x)}
    _L0_attn_a_in = _L0_attn_a_setup()

    def _L0_attn_b_setup():
        import jax, jax.numpy as jnp
        import numpy as np
        BSZ, SEQ, DZ = (4, 256, 128)
        C, R = (16, 64)
        SCALE = 0.03125
        REG_H = 1.0
        key = jax.random.key(seed)
        k1, k2, k3 = jax.random.split(key, 3)
        qz = jax.random.normal(k1, (BSZ, SEQ, DZ), dtype=jnp.float32)
        ternary_factor_u = jax.random.normal(k2, (C * R, DZ), dtype=jnp.float32) * 0.02
        ternary_factor_v = jax.random.normal(k3, (C * R, DZ), dtype=jnp.float32) * 0.02
        return {'qz': qz, 'ternary_factor_u': ternary_factor_u, 'ternary_factor_v': ternary_factor_v}
    _L0_attn_b_in = _L0_attn_b_setup()

    def _L0_ffn_setup():
        import jax, jax.numpy as jnp
        import numpy as np
        B, S, H = (8, 512, 128)
        NAV = 128
        E = 8
        F = 2 * H
        key = jax.random.key(seed)
        ks = jax.random.split(key, 12)

        def w(k, shape, fan_in):
            return jax.random.normal(k, shape, dtype=jnp.float32) / np.sqrt(fan_in)
        return {'hidden_states': jax.random.normal(ks[0], (B, S, H), dtype=jnp.float32), 'Wp1': w(ks[1], (H, NAV), H), 'bp1': jnp.zeros((NAV,), jnp.float32), 'Wp2': w(ks[2], (NAV, E), NAV), 'bp2': jnp.zeros((E,), jnp.float32), 'W1': w(ks[3], (E, H, F), H), 'b1': jnp.zeros((E, F), jnp.float32), 'W2': w(ks[4], (E, F, H), F), 'b2': jnp.zeros((E, H), jnp.float32), 'Wo': w(ks[5], (H, H), H), 'bo': jnp.zeros((H,), jnp.float32)}
    _L0_ffn_in = _L0_ffn_setup()
    _d = {'L0_attn_a_x': _L0_attn_a_in['x'], 'L0_attn_a_Win': _L0_attn_a_in['Win'], 'L0_attn_a_bin': _L0_attn_a_in['bin'], 'L0_attn_a_Wx': _L0_attn_a_in['Wx'], 'L0_attn_a_bx': _L0_attn_a_in['bx'], 'L0_attn_a_Wdt': _L0_attn_a_in['Wdt'], 'L0_attn_a_bdt': _L0_attn_a_in['bdt'], 'L0_attn_a_A_log': _L0_attn_a_in['A_log'], 'L0_attn_a_Dp': _L0_attn_a_in['Dp'], 'L0_attn_a_Wout': _L0_attn_a_in['Wout'], 'L0_attn_a_bout': _L0_attn_a_in['bout'], 'L0_attn_b_ternary_factor_u': _L0_attn_b_in['ternary_factor_u'], 'L0_attn_b_ternary_factor_v': _L0_attn_b_in['ternary_factor_v'], 'L0_ffn_Wp1': _L0_ffn_in['Wp1'], 'L0_ffn_bp1': _L0_ffn_in['bp1'], 'L0_ffn_Wp2': _L0_ffn_in['Wp2'], 'L0_ffn_bp2': _L0_ffn_in['bp2'], 'L0_ffn_W1': _L0_ffn_in['W1'], 'L0_ffn_b1': _L0_ffn_in['b1'], 'L0_ffn_W2': _L0_ffn_in['W2'], 'L0_ffn_b2': _L0_ffn_in['b2'], 'L0_ffn_Wo': _L0_ffn_in['Wo'], 'L0_ffn_bo': _L0_ffn_in['bo']}
    _x0 = _d['L0_attn_a_x']
    _d['L0_attn_a_x'] = jax.random.normal(jax.random.fold_in(jax.random.key(seed), 1), (8, 256, 128), dtype=_x0.dtype)
    del _x0
    return _d

def reference(L0_attn_a_x, L0_attn_a_Win, L0_attn_a_bin, L0_attn_a_Wx, L0_attn_a_bx, L0_attn_a_Wdt, L0_attn_a_bdt, L0_attn_a_A_log, L0_attn_a_Dp, L0_attn_a_Wout, L0_attn_a_bout, L0_attn_b_ternary_factor_u, L0_attn_b_ternary_factor_v, L0_ffn_Wp1, L0_ffn_bp1, L0_ffn_Wp2, L0_ffn_bp2, L0_ffn_W1, L0_ffn_b1, L0_ffn_W2, L0_ffn_b2, L0_ffn_Wo, L0_ffn_bo):

    def _L0_attn_a_ref(x, Win, bin, Wx, bx, Wdt, bdt, A_log, Dp, Wout, bout):
        import jax, jax.numpy as jnp
        import numpy as np
        D_MODEL, D_STATE, EXPAND = (128, 16, 2)
        D_INNER = D_MODEL * EXPAND
        DT_RANK = int(np.ceil(D_MODEL / 16))
        BATCH, SEQ = (2, 256)

        def _ssm_scan(xs, A, Bs, Cs, delta):
            batch, _, d_inner = xs.shape
            n = A.shape[1]

            def step(h, inp):
                x_t, d_t, B_t, C_t = inp
                dA = jnp.exp(d_t[:, :, None] * A)
                h = dA * h + (d_t * x_t)[:, :, None] * B_t[:, None, :]
                y = jnp.einsum('bdn,bn->bd', h, C_t)
                return (h, y)
            h0 = jnp.zeros((batch, d_inner, n), jnp.float32)
            inps = (xs.transpose(1, 0, 2), delta.transpose(1, 0, 2), Bs.transpose(1, 0, 2), Cs.transpose(1, 0, 2))
            _, ys = jax.lax.scan(step, h0, inps)
            return ys.transpose(1, 0, 2)

        def _reference_tuple_inner(x, Win, bin, Wx, bx, Wdt, bdt, A_log, Dp, Wout, bout):
            xz = x @ Win + bin
            xs, z = jnp.split(xz, 2, axis=-1)
            xs = jax.nn.silu(xs)
            xp = xs @ Wx + bx
            dp = xp[..., :DT_RANK]
            Bs = xp[..., DT_RANK:DT_RANK + D_STATE]
            Cs = xp[..., DT_RANK + D_STATE:]
            delta = jax.nn.softplus(dp @ Wdt + bdt)
            A = -jnp.exp(A_log.astype(jnp.float32))
            hidden = _ssm_scan(xs, A, Bs, Cs, delta)
            y = (hidden + xs * Dp) * jax.nn.silu(z)
            out = y @ Wout + bout
            return (out, hidden)
        return _reference_tuple_inner(x, Win, bin, Wx, bx, Wdt, bdt, A_log, Dp, Wout, bout)[0]

    def _L0_attn_b_ref(qz, ternary_factor_u, ternary_factor_v):
        import jax, jax.numpy as jnp
        import numpy as np
        BSZ, SEQ, DZ = (4, 256, 128)
        C, R = (16, 64)
        SCALE = 0.03125
        REG_H = 1.0
        bsz, seq_len, _ = qz.shape
        qz_u = qz @ ternary_factor_u.T * SCALE
        qz_v = qz @ ternary_factor_v.T * SCALE
        qz_u = qz_u.reshape(bsz, seq_len, C, R).transpose(0, 2, 1, 3)
        qz_v = qz_v.reshape(bsz, seq_len, C, R).transpose(0, 2, 1, 3)
        message_F = jnp.einsum('bcsr,bctr->bcst', qz_u, qz_v)
        qh = jax.nn.sigmoid(message_F / REG_H)
        qh_v1 = jnp.einsum('bcst,bctr->bcsr', qh, qz_v)
        qh_v2 = jnp.einsum('bcst,bcsr->bctr', qh, qz_u)
        qh_v1 = qh_v1.transpose(0, 2, 1, 3).reshape(bsz, seq_len, C * R)
        qh_v2 = qh_v2.transpose(0, 2, 1, 3).reshape(bsz, seq_len, C * R)
        message_G = (qh_v1 @ ternary_factor_u + qh_v2 @ ternary_factor_v) * SCALE
        return message_G

    def _L0_ffn_ref(hidden_states, Wp1, bp1, Wp2, bp2, W1, b1, W2, b2, Wo, bo):
        import jax, jax.numpy as jnp
        import numpy as np
        B, S, H = (8, 512, 128)
        NAV = 128
        E = 8
        F = 2 * H
        last = hidden_states[:, -1, :]
        logits = jax.nn.gelu(last @ Wp1 + bp1, approximate=False) @ Wp2 + bp2
        action_probs = jax.nn.softmax(logits, axis=-1)
        sel = jnp.argmax(action_probs, axis=-1)
        w1 = W1[sel]
        w2 = W2[sel]
        h = jax.nn.gelu(jnp.einsum('bsh,bhf->bsf', hidden_states, w1) + b1[sel][:, None, :], approximate=False)
        reasoned = jnp.einsum('bsf,bfh->bsh', h, w2) + b2[sel][:, None, :]
        out = reasoned @ Wo + bo
        return hidden_states + 0.3 * out
    x = L0_attn_a_x
    x = x + _L0_attn_a_ref(_layernorm(x, axis=-1), L0_attn_a_Win, L0_attn_a_bin, L0_attn_a_Wx, L0_attn_a_bx, L0_attn_a_Wdt, L0_attn_a_bdt, L0_attn_a_A_log, L0_attn_a_Dp, L0_attn_a_Wout, L0_attn_a_bout)
    x = x + _L0_ffn_ref(_layernorm(x, axis=-1), L0_ffn_Wp1, L0_ffn_bp1, L0_ffn_Wp2, L0_ffn_bp2, L0_ffn_W1, L0_ffn_b1, L0_ffn_W2, L0_ffn_b2, L0_ffn_Wo, L0_ffn_bo)
    x = x + _L0_attn_b_ref(_layernorm(x, axis=-1), L0_attn_b_ternary_factor_u, L0_attn_b_ternary_factor_v)
    x = x + _L0_ffn_ref(_layernorm(x, axis=-1), L0_ffn_Wp1, L0_ffn_bp1, L0_ffn_Wp2, L0_ffn_bp2, L0_ffn_W1, L0_ffn_b1, L0_ffn_W2, L0_ffn_b2, L0_ffn_Wo, L0_ffn_bo)
    return x

_drawn_inputs = setup_inputs


def setup_inputs(seed=0):
    import zlib

    import numpy as np

    out = dict(_drawn_inputs(seed))
    spreads = {'L0_ffn_bp1': (0.0, 0.8),
     'L0_ffn_bp2': (0.0, 0.8),
     'L0_ffn_b1': (0.0, 2.0),
     'L0_ffn_b2': (0.0, 2.0),
     'L0_ffn_bo': (0.0, 2.0)}
    factors = {'L0_attn_a_bin': 7.451,
     'L0_attn_a_Wx': 6.798,
     'L0_attn_a_bx': 8.0,
     'L0_attn_a_Wdt': 8.0,
     'L0_attn_a_bdt': 8.0,
     'L0_attn_a_A_log': 8.0,
     'L0_attn_b_ternary_factor_u': 64.0,
     'L0_attn_b_ternary_factor_v': 64.0,
     'L0_attn_a_Dp': 8.0,
     'L0_attn_a_bout': 43.679,
     'L0_ffn_Wp1': 8.0,
     'L0_ffn_Wp2': 8.0,
     'L0_ffn_W1': 8.0,
     'L0_ffn_W2': 8.0,
     'L0_ffn_Wo': 8.0}
    for name, (base, spread) in spreads.items():
        noise = np.random.default_rng([zlib.crc32(name.encode()), seed]).standard_normal(out[name].shape)
        drawn = base * np.exp(spread * noise) if base else spread * noise
        out[name] = jnp.asarray(drawn.astype(out[name].dtype))
    for name, factor in factors.items():
        out[name] = (out[name] * factor).astype(out[name].dtype)
    return out
```

```python
from contextlib import ExitStack

import concourse.bass as bass
from concourse import mybir

F32 = mybir.dt.float32
BF16 = mybir.dt.bfloat16
U32 = mybir.dt.uint32
U8 = mybir.dt.uint8
ALU = mybir.AluOpType
ACT = mybir.ActivationFunctionType
AX = mybir.AxisListType.X

P = 128
E_CONST = 2.718281828459045
LOG1P_SPLIT = 2.0 ** -7


def wait(eng, sem, value):
    if not isinstance(value, int) or value > 0:
        eng.wait_ge(sem, value)


class Chain:

    def __init__(self, eng, sem, base):
        self.eng, self.sem, self.count = eng, sem, base

    def __call__(self, instruction):
        self.count = self.count + 1
        instruction.then_inc(self.sem, 1)
        self.eng.wait_ge(self.sem, self.count)


def build(nc, x_in, Win, bin_, Wx, bx, Wdt, bdt, A_log, Dp, Wout, bout, Uf, Vf,
          Wp1, bp1, Wp2, bp2, W1, b1, W2, b2, Wo, bo, out):
    B, S, D = x_in.shape
    DI, NS = A_log.shape
    RK = Wdt.shape[0]
    KD = DI // P
    HB = B // 2
    HT = HB * S
    NBK = HT // 512
    CR = Uf.shape[0]
    NP = CR // P
    R = 64
    E, _, FH = W1.shape
    SB = S // P
    SCALE = 0.03125
    NIN = 2 * DI // P
    NBC = 2 * NS
    PARTS = 3 * NBC
    ROWS = NIN + 2 * KD + 4
    CB_BIN, CB_DT, CB_DP = 0, NIN, NIN + KD
    CB_BOUT, CB_BO, CB_BP1, CB_BX = ROWS - 4, ROWS - 3, ROWS - 2, ROWS - 1
    assert D == P and S == 256 and NP == 8 and KD == 2 and E == 8 and FH == 2 * P and NBK == 2
    RT_STEPS = 10

    with ExitStack() as ctx:
        def sb(name, shape, dt=F32):
            return ctx.enter_context(nc.sbuf_tensor(name, shape, dt))

        def sem(name):
            return ctx.enter_context(nc.semaphore(name))

        ps = ctx.enter_context(nc.psum_tensor("ps", [P, 8 * 512], F32))

        def bank(i, n=512, at=0):
            return ps[:, 512 * i + at:512 * i + at + n]

        x = sb("x", [P, B * S])
        hT = sb("hT", [P, B * S])
        hs = sb("hs", [P, 2 * HB * P])
        gT = sb("gT", [P, HT])
        ident = sb("ident", [P, P])
        sel32 = sb("sel32", [PARTS, NBC], BF16)
        sel = sb("sel", [PARTS, NBC, P], BF16)
        neghalf = sb("neghalf", [P, 2 * HB])
        econst = sb("econst", [1, HB * E])
        iota8 = sb("iota8", [1, E])
        eps = sb("eps", [P, 2 * HB])
        rows = sb("rows", [ROWS, P])
        cols = sb("cols", [P, ROWS])
        b12rows = sb("b12rows", [E, 3 * P])
        b12all = sb("b12all", [P, E, 3])
        win = sb("win", [P, 2 * DI])
        wx = sb("wx", [P, KD, PARTS + RK])
        wdt = sb("wdt", [PARTS + RK, DI])
        alog = sb("alog", [P, KD * NS])
        wout = sb("wout", [P, KD, P])
        unat = sb("unat", [P, NP, P])
        vnat = sb("vnat", [P, NP, P])
        uvfT = sb("uvfT", [P, 2, CR])
        wp1 = sb("wp1", [P, P])
        wp2 = sb("wp2", [P, E])
        bp2r = sb("bp2r", [1, E])
        wo = sb("wo", [P, P])
        negA = sb("negA", [P, KD * NS])
        diagD = sb("diagD", [P, KD, P])
        xs = sb("xs", [P, KD, HT])
        zs = sb("zs", [P, KD, HT])
        eb = sb("eb", [P, KD, HT])
        lnb = sb("lnb", [P, KD, HT])
        delta = sb("delta", [P, KD, HT])
        u = sb("u", [P, KD, HT])
        poly = sb("poly", [P, 2, HT])
        small = sb("small", [P, HT], U8)
        bcf = sb("bcf", [PARTS + RK, HT])
        res = sb("res", [PARTS, HT])
        parts = sb("parts", [PARTS, HT], BF16)
        mid = sb("mid", [PARTS, HT], BF16)
        dA = sb("dA", [P, 2, HB, S])
        dBu = sb("dBu", [P, 2, HT])
        h = sb("h", [P, 2, HT])
        hC = sb("hC", [P, 2, HT])
        Csb = sb("Csb", [P, 2, HT])
        yT = eb
        bo3 = sb("bo3", [P, 1])
        stats = sb("stats", [P, 2 * HB, 6])
        mv = sb("mv", [P, 2 * HB, 2])
        veps = sb("veps", [P, 2 * HB])
        rstd = sb("rstd", [P, 2 * HB])
        g1 = sb("g1", [P, HB])
        rt = sb("rt", [1, 6, HB, E])
        rs = sb("rs", [1, 6, HB])
        idx = sb("idx", [1, 2 * B], U32)
        w1s = sb("w1s", [P, 2, FH])
        w2s = sb("w2s", [P, 2, 2, P])
        b12s = sb("b12s", [P, B, 3])
        gf = sb("gf", [P, 2, 2, S])
        rT = sb("rT", [P, 2 * S])
        uvT = sb("uvT", [P, 2, 2 * S])
        nat = sb("nat", [P, 2, 4, P])
        tau = sb("tau", [P, 2, SB * S])
        qh = sb("qh", [P, 2, 2, SB, S])
        qhT = sb("qhT", [P, 2, SB, S])
        v12T = sb("v12T", [P, 2, 2 * S])

        ld_x = [sem(f"ld_x{i}") for i in range(2)]
        ld_rows, ld_mamba, ld_late, ld_scan = sem("ld_rows"), sem("ld_mamba"), sem("ld_late"), sem("ld_scan")
        k_pool, k_dve, k_rows, k_cols, k_b12, k_b12c = (
            sem("k_pool"), sem("k_dve"), sem("k_rows"), sem("k_cols"), sem("k_b12"), sem("k_b12c"))
        k_expA, k_uvf, k_uvfT = sem("k_expA"), sem("k_uvf"), sem("k_uvfT")
        fin_g, fin_gT, fin_xp, fin_x = sem("fin_g"), sem("fin_gT"), sem("fin_xp"), sem("fin_x")
        ln_stat, ln_mv, ln_eps, ln_rstd, ln_h, ln_xh, ln_tp, ln_hT = (
            sem("ln_stat"), sem("ln_mv"), sem("ln_eps"), sem("ln_rstd"), sem("ln_h"), sem("ln_xh"),
            sem("ln_tp"), sem("ln_hT"))
        rt_r1, rt_g, rt_r2, rt_d, rt_pow, rt_idx, rt_chain = (
            sem("rt_r1"), sem("rt_g"), sem("rt_r2"), sem("rt_d"), sem("rt_pow"), sem("rt_idx"),
            sem("rt_chain"))
        m_inp, m_silu, m_xp, m_bcf, m_parts, m_chain, m_dt, m_abs, m_e, m_ln, m_rel, m_u, m_y = (
            sem("m_inp"), sem("m_silu"), sem("m_xp"), sem("m_bcf"), sem("m_parts"), sem("m_chain"),
            sem("m_dt"), sem("m_abs"), sem("m_e"), sem("m_ln"), sem("m_rel"), sem("m_u"), sem("m_y"))
        s_B = [sem(f"s_B{r}") for r in range(2)]
        s_C = [sem(f"s_C{r}") for r in range(2)]
        s_Csb = [sem(f"s_Csb{r}") for r in range(2)]
        s_uB = [[sem(f"s_uB{r}{k}") for k in range(2)] for r in range(2)]
        s_dA = [[sem(f"s_dA{r}{k}") for k in range(2)] for r in range(2)]
        s_scan = [[sem(f"s_scan{r}{k}") for k in range(2)] for r in range(2)]
        s_hC = [[sem(f"s_hC{r}{k}") for k in range(2)] for r in range(2)]
        s_sum = [[sem(f"s_sum{r}{k}") for k in range(2)] for r in range(2)]
        w1_ld = [sem(f"w1_ld{s}") for s in range(2)]
        w2_ld = [sem(f"w2_ld{s}") for s in range(2)]
        f_h, f_g, f_r, f_rT = sem("f_h"), sem("f_g"), sem("f_r"), sem("f_rT")
        a_pr = [sem(f"a_pr{r}") for r in range(2)]
        a_uv = [sem(f"a_uv{r}") for r in range(2)]
        a_nt = [sem(f"a_nt{r}") for r in range(2)]
        a_nat = [sem(f"a_nat{r}") for r in range(2)]
        a_f = [sem(f"a_f{r}") for r in range(2)]
        a_tau = [[sem(f"a_tau{r}{i}") for i in range(2)] for r in range(2)]
        a_qh = [[sem(f"a_qh{r}{i}") for i in range(2)] for r in range(2)]
        a_t = [sem(f"a_t{r}") for r in range(2)]
        a_qhT = [sem(f"a_qhT{r}") for r in range(2)]
        a_pv = [sem(f"a_pv{r}") for r in range(2)]
        a_v12 = [sem(f"a_v12{r}") for r in range(2)]
        a_g = [sem(f"a_g{r}") for r in range(2)]
        pool_passed, dve_passed = sem("pool_passed"), sem("dve_passed")
        st_out = sem("st_out")

        xv = x[:].rearrange("p (b k d) -> p b k d", b=B, k=SB)
        x_dram = x_in.rearrange("b (k p) d -> p b k d", p=P)
        out_dram = out.rearrange("b (k p) d -> p b k d", p=P)
        hTv = hT[:].rearrange("p (b s) -> p b s", s=S)

        LN_A0, LN_A1, LN_F1, LN_AT = 0, 2, 4, 8
        FIN_A, FIN_F1, FIN_AT, FIN_F2 = 0, 2, 6, 14
        RT_A, RT_AT = 0, 2
        XH_A, XH_AT = 0, 2

        block = ctx.enter_context(nc.Block())

        def runtime(v):
            return not isinstance(v, int)

        def at(v, scale, n):
            return bass.ds(v * scale, n) if runtime(v) else slice(v * scale, v * scale + n)

        def prev_batch(b):
            return bass.ds(b * S - S, S) if runtime(b) else slice((b - 1) * S, b * S)

        snapped = {}

        def prepare(eng, b):
            snapped[eng.engine] = {c: eng.snap(4 * b + c) for c in range(6)} if runtime(b) else None

        def cnt(eng, b, p):
            c = p // 2 + 1
            return snapped[eng.engine][c] if runtime(b) else 4 * b + c

        @block.sync
        def _(sp):
            for g in range(2):
                sp.dma_start(xv[:, g * HB:(g + 1) * HB], x_dram[:, g * HB:(g + 1) * HB]).then_inc(ld_x[g], 16)
                if g == 0:
                    sp.dma_start(win[:], Win).then_inc(ld_mamba, 16)
            wx_v = Wx.rearrange("(k p) n -> p k n", p=P)
            for i in range(3):
                sp.dma_start(wx[:, :, i * NBC:(i + 1) * NBC], wx_v[:, :, RK:]).then_inc(ld_mamba, 16)
            sp.dma_start(wx[:, :, PARTS:], wx_v[:, :, 0:RK]).then_inc(ld_mamba, 16)
            sp.dma_start(wdt[PARTS:PARTS + RK, :], Wdt).then_inc(ld_mamba, 16)
            sp.dma_start(wout[:], Wout.rearrange("(k p) n -> p k n", p=P)).then_inc(ld_late, 16)
            sp.dma_start(wp1[:], Wp1).then_inc(ld_late, 16)
            sp.dma_start(wp2[:], Wp2).then_inc(ld_late, 16)
            sp.dma_start(bp2r[:], bp2.rearrange("(a e) -> a e", a=1)).then_inc(ld_late, 16)
            sp.dma_start(wo[:], Wo).then_inc(ld_late, 16)
            sp.dma_start(unat[:], Uf.rearrange("(c p) d -> p c d", p=P)).then_inc(ld_late, 16)
            sp.dma_start(vnat[:], Vf.rearrange("(c p) d -> p c d", p=P)).then_inc(ld_late, 16)

            def load_expert(f, i):
                j = 4 * f + i
                chosen = []
                for s in range(2):
                    wait(sp, rt_idx, (RT_A + 2 if runtime(i) or i >= 2 else RT_A + 1) if f == 0 else RT_AT + 2 * i + s + 1)
                    chosen.append(sp.value_load(idx[0:1, at(2 * i + (f * B + s), 1, 1)], min_val=0, max_val=E - 1))
                for s in range(2):
                    e = chosen[s]
                    wait(sp, f_h, 2 * j - 1 + s)
                    sp.dma_start(w1s[:, s, :], W1[bass.ds(e, 1), :, :].rearrange("a p n -> p (a n)")).then_inc(w1_ld[s], 16)
                    sp.dma_start(b12s[:, at(2 * i + s, 1, 1), :], b12all[:, bass.ds(e, 1), :]).then_inc(w1_ld[s], 16)
                for s in range(2):
                    wait(sp, f_r, 2 * j - 1 + s)
                    sp.dma_start(w2s[:, s, :, :], W2[bass.ds(chosen[s], 1), :, :].rearrange("a (c p) n -> p (a c) n", p=P))\
                        .then_inc(w2_ld[s], 16)

            sp.wait_ge(k_b12c, 1)
            load_expert(0, 0)
            with sp.Fori(1, 4) as i:
                load_expert(0, i)
            load_expert(1, 0)
            with sp.Fori(1, 4) as i:
                load_expert(1, i)
                sp.wait_ge(fin_x, FIN_F2 + i)
                sp.dma_start(out_dram[:, bass.ds(2 * i - 2, 2)], xv[:, bass.ds(2 * i - 2, 2)]).then_inc(st_out, 16)
            sp.wait_ge(fin_x, FIN_F2 + 4)
            sp.dma_start(out_dram[:, B - 2:B], xv[:, B - 2:B]).then_inc(st_out, 16)
            sp.wait_ge(st_out, 16 * 4)

        @block.gpsimd
        def _(pool):
            k = Chain(pool, k_pool, 0)
            k(pool.memset(ident[:], 0.0))
            k(pool.affine_select(out=ident[:], in_=ident[:], compare_op=ALU.not_equal, fill=1.0, base=0,
                                 pattern=[[-1, P]], channel_multiplier=1))
            k(pool.memset(sel32[:], 0.0))
            for i in range(3):
                k(pool.affine_select(out=sel32[:], in_=sel32[:], compare_op=ALU.not_equal, fill=1.0,
                                     base=-NBC * i, pattern=[[-1, NBC]], channel_multiplier=1))
            k(pool.tensor_copy(sel[:], sel32[:].unsqueeze(2).to_broadcast([PARTS, NBC, P])))
            k(pool.memset(neghalf[:], -0.5))
            k(pool.memset(econst[:], E_CONST))
            k(pool.memset(eps[:], 1e-5))
            k(pool.iota(iota8[:], pattern=[[1, E]], base=E, channel_multiplier=0, allow_small_or_imprecise_dtypes=True))

            def ln_rstd_(c, nb):
                n = SB * nb
                pool.wait_ge(ln_mv, c + 1)
                pool.tensor_tensor(veps[:, 0:n], mv[:, 0:n, 1], eps[:, 0:n], ALU.add).then_inc(ln_eps, 1)
                pool.wait_ge(ln_eps, c + 1)
                pool.tensor_tensor(rstd[:, 0:n], veps[:, 0:n], neghalf[:, 0:n], ALU.pow).then_inc(ln_rstd, 1)

            def rt_exp(r, nb):
                pool.wait_ge(rt_d, r + 1)
                pool.tensor_tensor(rt[:, 2, 0:nb], econst[:, 0:nb * E].rearrange("a (b e) -> a b e", e=E),
                                   rt[:, 1, 0:nb], ALU.pow).then_inc(rt_pow, 1)

            for g in range(2):
                ln_rstd_(LN_A0 + g, HB)

            def scan_step(J, r):
                for k in range(2):
                    pool.wait_ge(s_scan[r][k], J + 1)
                    if k == 0:
                        pool.wait_ge(s_Csb[r], J + 1)
                    wait(pool, s_sum[1 - r][k], J + r)
                    pool.tensor_tensor(hC[:, k], h[:, k], Csb[:, r], ALU.mult).then_inc(s_hC[r][k], 1)

            for g in range(2):
                J0 = g * NS // 2
                for r in range(2):
                    scan_step(J0, r)
                with pool.Fori(J0 + 1, J0 + NS // 2) as J:
                    for r in range(2):
                        scan_step(J, r)
                ln_rstd_(LN_A1 + g, HB)
                rt_exp(RT_A + g, HB)

            for i in range(4):
                ln_rstd_(LN_F1 + i, 2)

            def qh_step(b, p):
                for i in range(2):
                    pool.wait_ge(a_tau[p % 2][i], cnt(pool, b, p))
                    wait(pool, a_pv[p % 2], cnt(pool, b, p - 2))
                    pool.sem_inc(pool_passed, 1)
                    pool.tensor_scalar(qh[:, p % 2, i].rearrange("p k s -> p (k s)"), tau[:, i], 0.5, 0.5,
                                       ALU.mult, ALU.add).then_inc(a_qh[p % 2][i], 1)

            def batch(b, first=False, last=False):
                prepare(pool, b)
                for p in range(NP):
                    if not (last and p == NP - 1):
                        qh_step(b, p + 1)
                    if not first and p == 1:
                        ln_rstd_(LN_AT - 1 + b, 1)
                    if not first and p == 5:
                        rt_exp(RT_AT - 1 + b, 1)

            qh_step(0, 0)
            batch(0, first=True)
            with pool.Fori(1, B - 1) as b:
                batch(b)
            batch(B - 1, last=True)
            ln_rstd_(LN_AT + B - 1, 1)
            rt_exp(RT_AT + B - 1, 1)

        @block.scalar
        def _(act):
            act.dma_start(rows[0:NIN, :], bin_.rearrange("(c p) -> c p", p=P)).then_inc(ld_rows, 16)
            act.dma_start(rows[CB_DT:CB_DT + KD, :], bdt.rearrange("(c p) -> c p", p=P)).then_inc(ld_rows, 16)
            act.dma_start(rows[CB_DP:CB_DP + KD, :], Dp.rearrange("(c p) -> c p", p=P)).then_inc(ld_rows, 16)
            act.dma_start(rows[CB_BOUT:CB_BOUT + 1, :], bout.rearrange("(c p) -> c p", p=P)).then_inc(ld_rows, 16)
            act.dma_start(rows[CB_BO:CB_BO + 1, :], bo.rearrange("(c p) -> c p", p=P)).then_inc(ld_rows, 16)
            act.dma_start(rows[CB_BP1:CB_BP1 + 1, :], bp1.rearrange("(c p) -> c p", p=P)).then_inc(ld_rows, 16)
            bxr = bx.rearrange("(a n) -> a n", a=1)
            for i in range(3):
                act.dma_start(rows[CB_BX:CB_BX + 1, i * NBC:(i + 1) * NBC], bxr[:, RK:]).then_inc(ld_rows, 16)
            act.dma_start(rows[CB_BX:CB_BX + 1, PARTS:PARTS + RK], bxr[:, 0:RK]).then_inc(ld_rows, 16)
            act.dma_start(rows[CB_BX:CB_BX + 1, PARTS + RK:P], bxr[:, 0:P - PARTS - RK]).then_inc(ld_rows, 16)
            act.dma_start(b12rows[:, 0:FH], b1).then_inc(ld_rows, 16)
            act.dma_start(b12rows[:, FH:], b2).then_inc(ld_rows, 16)
            act.dma_start(alog[:].rearrange("p (k n) -> p k n", k=KD), A_log.rearrange("(k p) n -> p k n", p=P))\
                .then_inc(ld_scan, 16)

            def ln_copy(c, nb, tok, src):
                act.wait_ge(ln_tp, c + 1)
                act.activation(hT[:, tok], src, ACT.Copy).then_inc(ln_hT, 1)

            def fin_copy(f, nb, src, bias, scale):
                wait(act, fin_xp, f)
                act.activation(gT[:, 0:nb * S], src, ACT.Identity, bias=bias, scale=scale).then_inc(fin_gT, 1)

            def rt_gelu(r, nb, src):
                act.wait_ge(rt_r1, r + 1)
                act.activation(g1[:, 0:nb], src, ACT.Gelu, bias=cols[:, CB_BP1:CB_BP1 + 1]).then_inc(rt_g, 1)

            act.wait_ge(k_rows, 1)
            act.copy(cols[:], bank(7, ROWS)).then_inc(k_cols, 1)
            act.wait_ge(k_b12, 1)
            act.copy(b12all[:].rearrange("p e c -> p c e"), bank(6, 3 * E).rearrange("p (c e) -> p c e", e=E))\
                .then_inc(k_b12c, 1)
            act.wait_ge(ld_scan, 16)
            act.activation(negA[:], alog[:], ACT.Exp).then_inc(k_expA, 1)
            for g in range(2):
                ln_copy(LN_A0 + g, HB, slice(g * HT, (g + 1) * HT), ps[:, 4 * g * 512:4 * g * 512 + HT])
            act.wait_ge(k_cols, 1)

            def scan_step(J, r, j):
                for k in range(2):
                    wait(act, s_scan[1 - r][k], J + r)
                    n = k * NS + r + 2 * j
                    act.activation(dA[:, k, :, 1:], delta[:, k].rearrange("p (b s) -> p b s", s=S)[:, :, 1:],
                                   ACT.Exp, scale=negA[:, at(n, 1, 1)]).then_inc(s_dA[r][k], 1)
                act.wait_ge(s_C[r], J + 1)
                wait(act, s_hC[r][1], J)
                act.copy(Csb[:, r], ps[:, 2 * 512:2 * 512 + HT]).then_inc(s_Csb[r], 1)

            for g in range(2):
                for t in range(2 * NIN):
                    mc, nb = (t % 2) + 2 * (t // 4), (t // 2) % 2
                    dst = (xs if mc < KD else zs)[:, mc % KD, nb * 512:(nb + 1) * 512]
                    act.wait_ge(m_inp, 8 * g + t + 1)
                    act.activation(dst, bank(t % 4), ACT.Silu, bias=cols[:, CB_BIN + mc:CB_BIN + mc + 1])\
                        .then_inc(m_silu, 1)
                act.preload_act_table_set("natural_log_exp_and_others")
                for k in range(KD):
                    act.wait_ge(m_dt, 2 * g + k + 1)
                    act.activation(eb[:, k], ps[:, (4 + 2 * k) * 512:(6 + 2 * k) * 512], ACT.Abs,
                                   bias=cols[:, CB_DT + k:CB_DT + k + 1]).then_inc(m_abs, 1)
                for k in range(KD):
                    act.wait_ge(m_abs, 2 * g + k + 1)
                    act.activation(eb[:, k], eb[:, k], ACT.Exp, scale=-1.0).then_inc(m_e, 1)
                for k in range(KD):
                    act.wait_ge(m_e, 2 * g + k + 1)
                    act.activation(lnb[:, k], eb[:, k], ACT.Ln, bias=1.0).then_inc(m_ln, 1)
                act.wait_ge(m_u, 2 * g + 2)
                J0 = g * NS // 2
                for r in range(2):
                    scan_step(J0, r, 0)
                with act.Fori(1, NS // 2) as j:
                    for r in range(2):
                        scan_step(j + J0, r, j)
                act.wait_ge(fin_g, FIN_A + g + 1)
                fin_copy(FIN_A + g, HB, ps[:, 0:HT], cols[:, CB_BOUT:CB_BOUT + 1], 1.0)
                ln_copy(LN_A1 + g, HB, slice(g * HT, (g + 1) * HT), ps[:, 0:HT])
                rt_gelu(RT_A + g, HB, bank(2, HB))

            for i in range(4):
                act.wait_ge(k_uvf, i + 1)
                act.copy(uvfT[:, i // 2, (i % 2) * 512:(i % 2 + 1) * 512], bank(4 + i)).then_inc(k_uvfT, 1)

            def ffn_gelu(f, i):
                j = 4 * f + i
                for s in range(2):
                    wait(act, f_r, 2 * j - 1 + s)
                    act.wait_ge(f_h, 2 * j + s + 1)
                    for c in range(2):
                        ins = act.activation(gf[:, s, c], bank(s, S, c * S), ACT.Gelu,
                                             bias=b12s[:, at(2 * i + s, 1, 1), c])
                    ins.then_inc(f_g, 1)

            def ffn_fin(f, fi):
                act.wait_ge(fin_g, fi - (B if f else 0) + 1)
                fin_copy(fi, 2, bank(3), bo3[:, 0:1], 0.3)

            def ffn1_tail(i):
                ffn_fin(0, FIN_F1 + i)
                ln_copy(LN_F1 + i, 2, at(i, 2 * S, 2 * S), bank(7))

            ffn_gelu(0, 0)
            with act.Fori(1, 4) as i:
                ffn_fin(0, FIN_F1 + i - 1)
                ffn_gelu(0, i)
                ln_copy(LN_F1 + i - 1, 2, bass.ds(i * 2 * S - 2 * S, 2 * S), bank(7))
            ffn1_tail(3)

            def tanh_step(b, p):
                for i in range(2):
                    act.wait_ge(a_f[p % 2], cnt(act, b, p))
                    wait(act, a_qh[(p - 1) % 2][i], cnt(act, b, p - 1))
                    act.activation(tau[:, i], bank(i), ACT.Tanh, scale=0.5).then_inc(a_tau[p % 2][i], 1)

            def nat_step(b, p):
                act.wait_ge(a_nt[p % 2], cnt(act, b, p))
                wait(act, a_pv[p % 2], cnt(act, b, p - 2))
                act.copy(nat[:, p % 2].rearrange("p a c -> p (a c)"), bank(6)).then_inc(a_nat[p % 2], 1)

            def batch(b, first=False, last=False):
                prepare(act, b)
                for p in range(NP):
                    if not first:
                        if p == 3:
                            ln_copy(LN_AT - 1 + b, 1, prev_batch(b), bank(5, S))
                        if p == 4:
                            rt_gelu(RT_AT - 1 + b, 1, bank(5, 1))
                    if not (last and p == NP - 1):
                        tanh_step(b, p + 1)
                        nat_step(b, p + 1)
                    if not first and p == 0:
                        act.wait_ge(a_g[1], cnt(act, b, -1))
                        fin_copy(FIN_AT - 1 + b, 1, bank(7, S), 0.0, SCALE)

            tanh_step(0, 0)
            nat_step(0, 0)
            batch(0, first=True)
            with act.Fori(1, B - 1) as b:
                batch(b)
            batch(B - 1, last=True)
            act.wait_ge(a_g[1], cnt(act, B, -1))
            fin_copy(FIN_AT + B - 1, 1, bank(7, S), 0.0, SCALE)
            ln_copy(LN_AT + B - 1, 1, slice((B - 1) * S, B * S), bank(5, S))
            rt_gelu(RT_AT + B - 1, 1, bank(5, 1))

            ffn_gelu(1, 0)
            with act.Fori(1, 4) as i:
                ffn_fin(1, FIN_F2 + i - 1)
                ffn_gelu(1, i)
            ffn_fin(1, FIN_F2 + 3)

        @block.tensor
        def _(pe):
            def turn(dst, src, n=P):
                return pe.transpose(dst, src, ident[0:n, 0:n])

            def ln_turn(c, nb, dst):
                pe.wait_ge(ln_h, c + 1)
                for i in range(SB * nb):
                    ins = turn(dst[:, i * P:(i + 1) * P], hs[:, i * P:(i + 1) * P])
                ins.then_inc(ln_tp, 1)

            def fin_turn(f, nb, dst):
                pe.wait_ge(fin_gT, f + 1)
                for i in range(SB * nb):
                    ins = turn(dst[:, i * P:(i + 1) * P], gT[:, i * P:(i + 1) * P])
                ins.then_inc(fin_xp, 1)

            def rt_first(c, r, nb, b, dst):
                pe.wait_ge(ln_hT, c + 1)
                last = hTv[:, at(b, 1, nb), S - 1] if runtime(b) or nb == 1 else hTv[:, b:b + nb, S - 1]
                pe.matmul(dst[:, 0:nb], wp1[:], last, start=True, stop=True).then_inc(rt_r1, 1)

            def rt_second(r, nb, dst):
                pe.wait_ge(rt_g, r + 1)
                for i in range(nb):
                    ins = pe.matmul(dst[0:1, 64 + i * E:64 + (i + 1) * E], g1[:, i:i + 1], wp2[:], start=True, stop=True)
                ins.then_inc(rt_r2, 1)

            pe.wait_ge(k_pool, 2)
            pe.wait_ge(ld_rows, 16 * 13)
            turn(bank(7, ROWS), rows[:], ROWS).then_inc(k_rows, 1)
            for c in range(3):
                ins = turn(bank(6, E, c * E), b12rows[:, c * P:(c + 1) * P], E)
            ins.then_inc(k_b12, 1)
            for g in range(2):
                ln_turn(LN_A0 + g, HB, ps[:, 4 * g * 512:4 * g * 512 + HT])
            pe.wait_ge(ld_mamba, 16 * 6)

            def bcast(J, r, j, which):
                if which == 0:
                    wait(pe, s_uB[1 - r][1], J + r)
                else:
                    wait(pe, s_Csb[1 - r], J + r)
                row = which * NS + r + 2 * j
                for nb in range(NBK):
                    ins = pe.matmul(bank(2 * which + nb), sel[:, at(row, 1, 1), :].rearrange("q a m -> q (a m)"),
                                    parts[:, nb * 512:(nb + 1) * 512], start=True, stop=True)
                ins.then_inc((s_B if which == 0 else s_C)[r], 1)

            def add_up(J, r, stop=False):
                for k in range(2):
                    pe.wait_ge(s_hC[r][k], J + 1)
                    for nb in range(NBK):
                        ins = pe.matmul(bank(4 + 2 * k + nb), ident[:], hC[:, k, nb * 512:(nb + 1) * 512],
                                        start=False, stop=stop)
                    ins.then_inc(s_sum[r][k], 1)

            for g in range(2):
                pe.wait_ge(ln_hT, LN_A0 + 1 if g == 0 else LN_A1 + 1)
                if g:
                    pe.wait_ge(rt_d, RT_A + g)
                for t in range(2 * NIN):
                    mc, nb = (t % 2) + 2 * (t // 4), (t // 2) % 2
                    if t >= 4:
                        pe.wait_ge(m_silu, 8 * g + t - 3)
                    if t == 4 and g == 0:
                        pe.wait_ge(ln_hT, LN_A0 + 2)
                    pe.matmul(bank(t % 4), win[:, mc * P:(mc + 1) * P], hT[:, g * HT + nb * 512:g * HT + (nb + 1) * 512],
                              start=True, stop=True).then_inc(m_inp, 1)
                    if t in (4, 5):
                        nb = t - 4
                        pe.wait_ge(m_silu, 8 * g + 2 * nb + 2)
                        for k in range(KD):
                            ins = pe.matmul(ps[0:PARTS + RK, (4 + nb) * 512:(5 + nb) * 512], wx[:, k, :],
                                            xs[:, k, nb * 512:(nb + 1) * 512], start=(k == 0), stop=(k == KD - 1))
                        ins.then_inc(m_xp, 1)
                for k in range(KD):
                    for nb in range(NBK):
                        pe.wait_ge(m_bcf, 2 * g + NBK)
                        ins = pe.matmul(bank(4 + 2 * k + nb), wdt[PARTS:PARTS + RK, k * P:(k + 1) * P],
                                        bcf[PARTS:PARTS + RK, nb * 512:(nb + 1) * 512], start=True, stop=True)
                    ins.then_inc(m_dt, 1)
                pe.wait_ge(m_parts, g + 1)
                J0 = g * NS // 2
                pe.wait_ge(m_silu, 8 * g + 8)
                pe.wait_ge(k_pool, 7)
                for which in range(2):
                    bcast(J0, 0, 0, which)
                pe.wait_ge(k_dve, 3)
                for k in range(KD):
                    pe.wait_ge(m_abs, 2 * g + k + 1)
                    pe.wait_ge(m_rel, 2 * g + k + 1)
                    for nb in range(NBK):
                        pe.matmul(bank(4 + 2 * k + nb), diagD[:, k, :], xs[:, k, nb * 512:(nb + 1) * 512],
                                  start=True, stop=False)
                for which in range(2):
                    bcast(J0, 1, 0, which)
                add_up(J0, 0)
                with pe.Fori(1, NS // 2) as j:
                    J = pe.snap(j + J0)
                    for which in range(2):
                        bcast(J, 0, j, which)
                    add_up(J - 1, 1)
                    for which in range(2):
                        bcast(J, 1, j, which)
                    add_up(J, 0)
                add_up(J0 + NS // 2 - 1, 1, stop=True)
                pe.wait_ge(ld_late, 16 * 7)
                for nb in range(NBK):
                    for k in range(KD):
                        pe.wait_ge(m_y, 2 * g + k + 1)
                        ins = pe.matmul(bank(nb), wout[:, k, :], yT[:, k, nb * 512:(nb + 1) * 512],
                                        start=(k == 0), stop=(k == KD - 1))
                ins.then_inc(fin_g, 1)
                fin_turn(FIN_A + g, HB, ps[:, 2 * 512:2 * 512 + HT])
                ln_turn(LN_A1 + g, HB, ps[:, 0:HT])
                rt_first(LN_A1 + g, RT_A + g, HB, g * HB, bank(2))
                rt_second(RT_A + g, HB, bank(2))

            for i in range(4):
                src = unat if i < 2 else vnat
                for c in range(4):
                    ins = turn(bank(4 + i, P, c * P), src[:, 4 * (i % 2) + c, :])
                ins.then_inc(k_uvf, 1)
            pe.wait_ge(k_uvfT, 4)
            pe.wait_ge(rt_d, RT_A + 2)

            def ffn_hidden(f, i):
                j = 4 * f + i
                for s in range(2):
                    pe.wait_ge(w1_ld[s], 32 * j + 32)
                    wait(pe, f_g, 2 * j - 1 + s)
                    for c in range(2):
                        ins = pe.matmul(bank(s, S, c * S), w1s[:, s, c * P:(c + 1) * P],
                                        hT[:, bass.ds(i * 2 * S + s * S, S) if runtime(i) else slice((2 * i + s) * S, (2 * i + s + 1) * S)],
                                        start=True, stop=True)
                    ins.then_inc(f_h, 1)

            def ffn_second(f, i):
                j = 4 * f + i
                for s in range(2):
                    pe.wait_ge(w2_ld[s], 16 * j + 16)
                    wait(pe, f_rT, 2 * j - 1 + s)
                    pe.wait_ge(f_g, 2 * j + s + 1)
                    for c in range(2):
                        ins = pe.matmul(bank(2 + 3 * s, S), w2s[:, s, c, :], gf[:, s, c], start=(c == 0), stop=(c == 1))
                    ins.then_inc(f_r, 1)

            def ffn_out(f, i):
                pe.wait_ge(f_rT, 2 * (4 * f + i) + 2)
                pe.matmul(bank(3), wo[:], rT[:], start=True, stop=True).then_inc(fin_g, 1)

            ffn_hidden(0, 0)
            ffn_second(0, 0)
            ffn_out(0, 0)
            with pe.Fori(1, 4) as i:
                ffn_hidden(0, i)
                fin_turn(FIN_F1 - 1 + i, 2, bank(4))
                ffn_second(0, i)
                ln_turn(LN_F1 - 1 + i, 2, bank(7))
                ffn_out(0, i)

            def project(b, p):
                tok = b if not runtime(b) else b
                off = p // NP
                src = hT[:, bass.ds(b * S + off * S, S) if runtime(b) else slice((b + off) * S, (b + off + 1) * S)]
                wait(pe, a_uv[(p - 1) % 2], cnt(pe, b, p - 1))
                for w in range(2):
                    ins = pe.matmul(bank(5, S, w * S), uvfT[:, w, (p % NP) * P:(p % NP + 1) * P], src,
                                    start=True, stop=True)
                ins.then_inc(a_pr[p % 2], 1)

            def messages(b, p):
                pe.wait_ge(a_uv[p % 2], cnt(pe, b, p))
                wait(pe, a_tau[(p - 1) % 2][1], cnt(pe, b, p - 1))
                for k in range(SB):
                    for i in range(2):
                        ins = pe.matmul(bank(i, S, k * S), uvT[i * R:(i + 1) * R, p % 2, k * P:(k + 1) * P],
                                        uvT[i * R:(i + 1) * R, p % 2, S:2 * S], start=True, stop=True)
                ins.then_inc(a_f[p % 2], 1)

            def turn_uv(b, p):
                pe.wait_ge(a_uv[p % 2], cnt(pe, b, p))
                wait(pe, a_nat[(p - 1) % 2], cnt(pe, b, p - 1))
                for i in range(4):
                    ins = turn(bank(6, P, i * P), uvT[:, p % 2, i * P:(i + 1) * P])
                ins.then_inc(a_nt[p % 2], 1)

            def turn_qh(b, p):
                wait(pe, a_qhT[(p - 1) % 2], cnt(pe, b, p - 1))
                for i in range(2):
                    pe.wait_ge(a_qh[p % 2][i], cnt(pe, b, p))
                    for k in range(SB):
                        for t in range(SB):
                            ins = turn(bank(2 + i, P, t * S + k * P), qh[:, p % 2, i, k, t * P:(t + 1) * P])
                ins.then_inc(a_t[p % 2], 1)

            def qhT_u(b, p):
                pe.wait_ge(a_nat[p % 2], cnt(pe, b, p))
                wait(pe, a_v12[(p - 1) % 2], cnt(pe, b, p - 1))
                for k in range(SB):
                    for i in range(2):
                        pe.matmul(ps[i * R:(i + 1) * R, 4 * 512 + S:5 * 512], nat[:, p % 2, k, i * R:(i + 1) * R],
                                  qh[:, p % 2, i, k, :], start=(k == 0), stop=(k == SB - 1))

            def qh_v(b, p):
                pe.wait_ge(a_qhT[p % 2], cnt(pe, b, p))
                for t in range(SB):
                    for i in range(2):
                        ins = pe.matmul(ps[i * R:(i + 1) * R, 4 * 512:4 * 512 + S], nat[:, p % 2, SB + t, i * R:(i + 1) * R],
                                        qhT[:, i, t, :], start=(t == 0), stop=(t == SB - 1))
                ins.then_inc(a_pv[p % 2], 1)

            def sum_pair(b, p):
                pe.wait_ge(a_v12[p % 2], cnt(pe, b, p))
                for w, nat_w in enumerate((unat, vnat)):
                    ins = pe.matmul(bank(7, S), nat_w[:, p % NP, :], v12T[:, p % 2, w * S:(w + 1) * S],
                                    start=(p % NP == 0 and w == 0), stop=(p % NP == NP - 1 and w == 1))
                ins.then_inc(a_g[p % 2], 1)

            def batch(b, first=False, last=False):
                prepare(pe, b)
                for p in range(NP):
                    if not first:
                        if p in (1, 3, 4, 5):
                            pe.wait_ge(a_uv[(p + 1) % 2], cnt(pe, b, p + 1))
                        if p == 1:
                            fin_turn(FIN_AT - 1 + b, 1, bank(5, S))
                        if p == 3:
                            ln_turn(LN_AT - 1 + b, 1, bank(5, S))
                        if p == 4:
                            rt_first(LN_AT - 1 + b, RT_AT - 1 + b, 1, b - 1, bank(5))
                        if p == 5:
                            rt_second(RT_AT - 1 + b, 1, bank(5))
                    if not (last and p == NP - 1):
                        messages(b, p + 1)
                    turn_qh(b, p)
                    qhT_u(b, p)
                    if not (first and p == 0):
                        sum_pair(b, p - 1)
                    if not (last and p >= NP - 2):
                        if not first:
                            if p == 1:
                                pe.wait_ge(fin_x, FIN_AT + b)
                            if p == 3:
                                pe.wait_ge(ln_hT, LN_AT + b)
                            if p == 4:
                                pe.wait_ge(rt_g, RT_AT + b)
                            if p == 5:
                                pe.wait_ge(rt_d, RT_AT + b)
                        project(b, p + 2)
                    qh_v(b, p)
                    if not (last and p == NP - 1):
                        turn_uv(b, p + 1)

            fin_turn(FIN_F1 + 3, 2, bank(4))
            project(0, 0)
            ln_turn(LN_F1 + 3, 2, bank(7))
            project(0, 1)
            messages(0, 0)
            turn_uv(0, 0)
            pe.wait_ge(ln_hT, LN_F1 + 4)
            batch(0, first=True)
            with pe.Fori(1, B - 1) as b:
                batch(b)
            batch(B - 1, last=True)
            sum_pair(B - 1, NP - 1)
            fin_turn(FIN_AT + B - 1, 1, bank(5, S))
            pe.wait_ge(fin_x, FIN_AT + B)
            ln_turn(LN_AT + B - 1, 1, bank(5, S))
            rt_first(LN_AT + B - 1, RT_AT + B - 1, 1, B - 1, bank(5))
            rt_second(RT_AT + B - 1, 1, bank(5))
            pe.wait_ge(rt_d, RT_AT + B)

            ffn_hidden(1, 0)
            ffn_second(1, 0)
            ffn_out(1, 0)
            with pe.Fori(1, 4) as i:
                ffn_hidden(1, i)
                fin_turn(FIN_F2 - 1 + i, 2, bank(4))
                ffn_second(1, i)
                ffn_out(1, i)
            fin_turn(FIN_F2 + 3, 2, bank(4))

        @block.vector
        def _(dve):
            def ln_stats(c, nb, blk):
                for i in range(SB * nb):
                    ins = dve.bn_stats(stats[:, i, :], x[:, blk(i)])
                ins.then_inc(ln_stat, 1)
                wait(dve, ln_h, c)
                dve.wait_ge(ln_stat, c + 1)
                dve.sem_inc(dve_passed, 1)
                for i in range(SB * nb):
                    ins = dve.bn_aggr(mv[:, i, :], stats[:, i, :])
                ins.then_inc(ln_mv, 1)

            def ln_norm(c, nb, blk, xh=None):
                wait(dve, ln_tp, c)
                dve.wait_ge(ln_rstd, c + 1)
                for i in range(SB * nb):
                    ins = dve.tensor_scalar(hs[:, i * P:(i + 1) * P], x[:, blk(i)], mv[:, i, 0:1], rstd[:, i:i + 1],
                                            ALU.subtract, ALU.mult)
                ins.then_inc(ln_h, 1)
                if xh is not None:
                    dve.wait_ge(ln_h, c + 1)
                    whole = blk(0, SB * nb)
                    dve.tensor_tensor(x[:, whole], x[:, whole], hs[:, 0:SB * nb * P], ALU.add).then_inc(ln_xh, 1)

            def fin_add(f, nb, tok, src):
                dve.wait_ge(fin_xp, f + 1)
                dve.tensor_tensor(x[:, tok], src, x[:, tok], ALU.add).then_inc(fin_x, 1)
                dve.wait_ge(fin_x, f + 1)

            def rt_logits(r, nb, src):
                k = Chain(dve, rt_chain, r * RT_STEPS)
                dve.wait_ge(rt_r2, r + 1)
                k(dve.tensor_tensor(rt[:, 0, 0:nb], src[0:1, 64:64 + nb * E].rearrange("a (b e) -> a b e", e=E),
                                    bp2r[:].unsqueeze(1).to_broadcast([1, nb, E]), ALU.add))
                k(dve.tensor_reduce(rs[:, 0, 0:nb], rt[:, 0, 0:nb], AX, ALU.max))
                dve.tensor_tensor(rt[:, 1, 0:nb], rt[:, 0, 0:nb], rs[:, 0, 0:nb].unsqueeze(2).to_broadcast([1, nb, E]),
                                  ALU.subtract).then_inc(rt_d, 1)

            def rt_choose(r, nb, col):
                k = Chain(dve, rt_chain, r * RT_STEPS + 2)
                dve.wait_ge(rt_pow, r + 1)
                k(dve.tensor_reduce(rs[:, 1, 0:nb], rt[:, 2, 0:nb], AX, ALU.add))
                k(dve.reciprocal(rs[:, 2, 0:nb], rs[:, 1, 0:nb]))
                k(dve.tensor_tensor(rt[:, 3, 0:nb], rt[:, 2, 0:nb], rs[:, 2, 0:nb].unsqueeze(2).to_broadcast([1, nb, E]),
                                    ALU.mult))
                k(dve.tensor_reduce(rs[:, 3, 0:nb], rt[:, 3, 0:nb], AX, ALU.max))
                k(dve.tensor_tensor(rt[:, 4, 0:nb], rt[:, 3, 0:nb], rs[:, 3, 0:nb].unsqueeze(2).to_broadcast([1, nb, E]),
                                    ALU.is_ge))
                k(dve.tensor_scalar(rt[:, 4, 0:nb], rt[:, 4, 0:nb], -float(E), None, ALU.mult))
                k(dve.tensor_tensor(rt[:, 5, 0:nb], rt[:, 4, 0:nb], iota8[:].unsqueeze(1).to_broadcast([1, nb, E]), ALU.add))
                k(dve.tensor_reduce(rs[:, 4, 0:nb], rt[:, 5, 0:nb], AX, ALU.min))
                dve.tensor_copy(idx[:, col], rs[:, 4, 0:nb]).then_inc(rt_idx, 1)

            def blocks(start, scale=1):
                def blk(i, n=1):
                    if runtime(start):
                        return bass.ds(start * P + i * P, n * P)
                    return slice((start + i) * P, (start + i + n) * P)
                return blk

            dve.memset(dA[:, :, :, 0], 0.0).then_inc(k_dve, 1)
            for g in range(2):
                dve.wait_ge(ld_x[g], 16)
                ln_stats(LN_A0 + g, HB, blocks(g * 2 * HB))
                ln_norm(LN_A0 + g, HB, blocks(g * 2 * HB))
            dve.wait_ge(k_cols, 1)
            dve.wait_ge(k_pool, 11)
            dve.tensor_scalar(bo3[:], cols[:, CB_BO:CB_BO + 1], 0.3, None, ALU.mult).then_inc(k_dve, 1)
            for k in range(KD):
                ins = dve.tensor_scalar(diagD[:, k, :], ident[:], cols[:, CB_DP + k:CB_DP + k + 1], None, ALU.mult)
            ins.then_inc(k_dve, 1)
            dve.wait_ge(k_expA, 1)
            dve.tensor_scalar(negA[:], negA[:], -1.0, None, ALU.mult).then_inc(k_dve, 1)

            def scan_step(J, r):
                for k in range(2):
                    if k == 0:
                        dve.wait_ge(s_B[r], J + 1)
                    wait(dve, s_scan[1 - r][k], J + r)
                    dve.tensor_tensor(dBu[:, k], ps[:, 0:HT], u[:, k], ALU.mult).then_inc(s_uB[r][k], 1)
                for k in range(2):
                    dve.wait_ge(s_dA[r][k], J + 1)
                    dve.wait_ge(s_uB[r][k], J + 1)
                    wait(dve, s_hC[1 - r][k], J + r)
                    dve.tensor_tensor_scan(h[:, k], dA[:, k].rearrange("p b s -> p (b s)"), dBu[:, k], 0.0,
                                           ALU.mult, ALU.add).then_inc(s_scan[r][k], 1)

            FRONT = 18
            for g in range(2):
                k_ = Chain(dve, m_chain, g * FRONT)
                for nb in range(NBK):
                    dve.wait_ge(m_xp, 2 * g + nb + 1)
                    dve.tensor_scalar(bcf[:, nb * 512:(nb + 1) * 512], ps[0:PARTS + RK, (4 + nb) * 512:(5 + nb) * 512],
                                      cols[0:PARTS + RK, CB_BX:CB_BX + 1], None, ALU.add).then_inc(m_bcf, 1)
                dve.wait_ge(m_bcf, 2 * g + 2)
                k_(dve.tensor_copy(parts[:], bcf[0:PARTS, :]))
                k_(dve.tensor_tensor(res[:], bcf[0:PARTS, :], parts[:], ALU.subtract))
                k_(dve.tensor_copy(mid[2 * NBC:PARTS, :], res[2 * NBC:PARTS, :]))
                k_(dve.tensor_copy(parts[NBC:2 * NBC, :], res[NBC:2 * NBC, :]))
                dve.tensor_tensor(parts[2 * NBC:PARTS, :], res[2 * NBC:PARTS, :], mid[2 * NBC:PARTS, :], ALU.subtract)\
                    .then_inc(m_parts, 1)
                for k in range(KD):
                    dve.wait_ge(m_abs, 2 * g + k + 1)
                    dve.tensor_scalar(delta[:, k], ps[:, (4 + 2 * k) * 512:(6 + 2 * k) * 512],
                                      cols[:, CB_DT + k:CB_DT + k + 1], 0.0, ALU.add, ALU.max).then_inc(m_rel, 1)
                for k in range(KD):
                    dve.wait_ge(m_e, 2 * g + k + 1)
                    e = eb[:, k]
                    k_(dve.tensor_scalar(small[:], e, LOG1P_SPLIT, None, ALU.is_lt))
                    k_(dve.tensor_scalar(poly[:, 0], e, 1.0 / 3.0, -0.5, ALU.mult, ALU.add))
                    k_(dve.tensor_tensor(poly[:, 1], poly[:, 0], e, ALU.mult))
                    k_(dve.scalar_tensor_tensor(out=poly[:, 0], in0=poly[:, 1], scalar=1.0, in1=e, op0=ALU.add,
                                                op1=ALU.mult))
                    dve.wait_ge(m_ln, 2 * g + k + 1)
                    k_(dve.copy_predicated(lnb[:, k], small[:], poly[:, 0]))
                    k_(dve.tensor_tensor(delta[:, k], delta[:, k], lnb[:, k], ALU.add))
                    k_(dve.tensor_tensor(u[:, k], delta[:, k], xs[:, k], ALU.mult))
                    dve.sem_inc(m_u, 1)
                J0 = g * NS // 2
                for r in range(2):
                    scan_step(J0, r)
                with dve.Fori(J0 + 1, J0 + NS // 2) as J:
                    for r in range(2):
                        scan_step(J, r)
                for k in range(KD):
                    dve.wait_ge(s_sum[1][k], J0 + NS // 2)
                    dve.tensor_tensor(yT[:, k], ps[:, (4 + 2 * k) * 512:(6 + 2 * k) * 512], zs[:, k], ALU.mult)\
                        .then_inc(m_y, 1)
                fin_add(FIN_A + g, HB, slice(g * HT, (g + 1) * HT), ps[:, 2 * 512:2 * 512 + HT])
                ln_stats(LN_A1 + g, HB, blocks(g * 2 * HB))
                ln_norm(LN_A1 + g, HB, blocks(g * 2 * HB), xh=XH_A + g)
                if g == 0:
                    dve.wait_ge(ld_late, 16 * 7)
                rt_logits(RT_A + g, HB, bank(2))
                rt_choose(RT_A + g, HB, slice(g * HB, (g + 1) * HB))

            def ffn_bias(f, i):
                j = 4 * f + i
                for s in range(2):
                    if s == 0:
                        wait(dve, fin_g, 2 + j)
                    dve.wait_ge(f_r, 2 * j + s + 1)
                    dve.tensor_scalar(rT[:, s * S:(s + 1) * S], bank(2 + 3 * s, S), b12s[:, at(2 * i + s, 1, 1), 2],
                                      None, ALU.add).then_inc(f_rT, 1)

            ffn_bias(0, 0)
            dve.wait_ge(ln_xh, XH_A + 2)
            with dve.Fori(1, 4) as i:
                fin_add(FIN_F1 - 1 + i, 2, bass.ds(i * 2 * S - 2 * S, 2 * S), bank(4))
                ln_stats(LN_F1 - 1 + i, 2, blocks(i * 4 - 4))
                ffn_bias(0, i)
                ln_norm(LN_F1 - 1 + i, 2, blocks(i * 4 - 4))
            fin_add(FIN_F1 + 3, 2, slice(6 * S, 8 * S), bank(4))
            ln_stats(LN_F1 + 3, 2, blocks(12))

            def uv_step(b, p):
                wait(dve, a_f[p % 2], cnt(dve, b, p - 2))
                wait(dve, a_nt[p % 2], cnt(dve, b, p - 2))
                dve.wait_ge(a_pr[p % 2], cnt(dve, b, p))
                dve.tensor_scalar(uvT[:, p % 2], bank(5), SCALE, None, ALU.mult).then_inc(a_uv[p % 2], 1)

            def batch(b, first=False, last=False):
                prepare(dve, b)
                prev = blocks(b * 2 - 2)
                for p in range(NP):
                    if not first and p == 1:
                        fin_add(FIN_AT - 1 + b, 1, prev_batch(b), bank(5, S))
                    wait(dve, a_pv[(p - 1) % 2], cnt(dve, b, p - 1))
                    dve.wait_ge(a_t[p % 2], cnt(dve, b, p))
                    for i in range(2):
                        ins = dve.tensor_copy(qhT[:, i].rearrange("p k s -> p (k s)"), bank(2 + i))
                    ins.then_inc(a_qhT[p % 2], 1)
                    if not first:
                        if p == 1:
                            ln_stats(LN_AT - 1 + b, 1, prev)
                        if p == 2:
                            ln_norm(LN_AT - 1 + b, 1, prev, xh=True)
                        if p == 5:
                            rt_logits(RT_AT - 1 + b, 1, bank(5))
                        if p == 6:
                            rt_choose(RT_AT - 1 + b, 1, bass.ds(b + (B - 1), 1) if runtime(b) else slice(B + b - 1, B + b))
                    if not (last and p >= NP - 2):
                        uv_step(b, p + 2)
                    wait(dve, a_g[p % 2], cnt(dve, b, p - 2))
                    dve.wait_ge(a_pv[p % 2], cnt(dve, b, p))
                    dve.tensor_copy(v12T[:, p % 2], bank(4)).then_inc(a_v12[p % 2], 1)

            uv_step(0, 0)
            ln_norm(LN_F1 + 3, 2, blocks(12))
            uv_step(0, 1)
            batch(0, first=True)
            with dve.Fori(1, B - 1) as b:
                batch(b)
            batch(B - 1, last=True)
            fin_add(FIN_AT + B - 1, 1, slice((B - 1) * S, B * S), bank(5, S))
            ln_stats(LN_AT + B - 1, 1, blocks(2 * B - 2))
            ln_norm(LN_AT + B - 1, 1, blocks(2 * B - 2), xh=True)
            rt_logits(RT_AT + B - 1, 1, bank(5))
            rt_choose(RT_AT + B - 1, 1, slice(2 * B - 1, 2 * B))

            ffn_bias(1, 0)
            dve.wait_ge(ln_xh, XH_AT + B)
            with dve.Fori(1, 4) as i:
                fin_add(FIN_F2 - 1 + i, 2, bass.ds(i * 2 * S - 2 * S, 2 * S), bank(4))
                ffn_bias(1, i)
            fin_add(FIN_F2 + 3, 2, slice(6 * S, 8 * S), bank(4))


_INS = ['L0_attn_a_x', 'L0_attn_a_Win', 'L0_attn_a_bin', 'L0_attn_a_Wx', 'L0_attn_a_bx', 'L0_attn_a_Wdt',
        'L0_attn_a_bdt', 'L0_attn_a_A_log', 'L0_attn_a_Dp', 'L0_attn_a_Wout', 'L0_attn_a_bout',
        'L0_attn_b_ternary_factor_u', 'L0_attn_b_ternary_factor_v', 'L0_ffn_Wp1', 'L0_ffn_bp1', 'L0_ffn_Wp2',
        'L0_ffn_bp2', 'L0_ffn_W1', 'L0_ffn_b1', 'L0_ffn_W2', 'L0_ffn_b2', 'L0_ffn_Wo', 'L0_ffn_bo']


def kernel(**inputs):
    import numpy as np
    import concourse.bacc as bacc
    from concourse.bass_utils import run_bass_kernel_spmd

    nc = bacc.Bacc("TRN2", target_bir_lowering=False, num_devices=1)
    arrays, args = {}, []
    for name in _INS:
        a = np.ascontiguousarray(inputs[name])
        arrays[f"in_{name}"] = a
        args.append(nc.dram_tensor(f"in_{name}", a.shape, mybir.dt.from_np(a.dtype), kind="ExternalInput").ap())
    out = nc.dram_tensor("out_x", inputs['L0_attn_a_x'].shape, F32, kind="ExternalOutput").ap()
    build(nc, *args, out)
    result = run_bass_kernel_spmd(nc, [arrays], core_ids=[0])
    return result.results[0]["out_x"]
```

```python
from contextlib import ExitStack

import concourse.bass as bass
from concourse import mybir

F32 = mybir.dt.float32
BF16 = mybir.dt.bfloat16
F32R = mybir.dt.float32r
U32 = mybir.dt.uint32
U8 = mybir.dt.uint8
ALU = mybir.AluOpType
ACT = mybir.ActivationFunctionType
AX = mybir.AxisListType.X

P = 128
E_CONST = 2.718281828459045
LOG1P_SPLIT = 2.0 ** -7


def wait(eng, sem, value):
    if not isinstance(value, int) or value > 0:
        eng.wait_ge(sem, value)


class Chain:

    def __init__(self, eng, sem, base):
        self.eng, self.sem, self.count = eng, sem, base

    def __call__(self, instruction):
        self.count = self.count + 1
        instruction.then_inc(self.sem, 1)
        self.eng.wait_ge(self.sem, self.count)


def build(nc, x_in, Win, bin_, Wx, bx, Wdt, bdt, A_log, Dp, Wout, bout, Uf, Vf,
          Wp1, bp1, Wp2, bp2, W1, b1, W2, b2, Wo, bo, out):
    B, S, D = x_in.shape
    DI, NS = A_log.shape
    RK = Wdt.shape[0]
    KD = DI // P
    HB = B // 2
    HT = HB * S
    NBK = HT // 512
    CR = Uf.shape[0]
    NP = CR // P
    R = 64
    E, _, FH = W1.shape
    SB = S // P
    SCALE = 0.03125
    NIN = 2 * DI // P
    NBC = 2 * NS
    PARTS = 3 * NBC
    ROWS = NIN + 2 * KD + 4
    CB_BIN, CB_DT, CB_DP = 0, NIN, NIN + KD
    CB_BOUT, CB_BO, CB_BP1, CB_BX = ROWS - 4, ROWS - 3, ROWS - 2, ROWS - 1
    assert D == P and S == 256 and NP == 8 and KD == 2 and E == 8 and FH == 2 * P and NBK == 2
    RT_STEPS = 10

    with ExitStack() as ctx:
        def sb(name, shape, dt=F32):
            return ctx.enter_context(nc.sbuf_tensor(name, shape, dt))

        def sem(name):
            return ctx.enter_context(nc.semaphore(name))

        ps = ctx.enter_context(nc.psum_tensor("ps", [P, 8 * 512], F32))

        def bank(i, n=512, at=0):
            return ps[:, 512 * i + at:512 * i + at + n]

        x = sb("x", [P, B * S])
        hT = sb("hT", [P, B * S])
        hs = sb("hs", [P, 2 * HB * P])
        gT = sb("gT", [P, HT])
        ident = sb("ident", [P, P])
        sel32 = sb("sel32", [PARTS, NBC], BF16)
        sel = sb("sel", [PARTS, NBC, P], BF16)
        neghalf = sb("neghalf", [P, 2 * HB])
        econst = sb("econst", [1, HB * E])
        iota8 = sb("iota8", [1, E])
        eps = sb("eps", [P, 2 * HB])
        rows = sb("rows", [ROWS, P])
        cols = sb("cols", [P, ROWS])
        b12rows = sb("b12rows", [E, 3 * P])
        b12all = sb("b12all", [P, E, 3])
        win = sb("win", [P, 2 * DI])
        wx = sb("wx", [P, KD, PARTS + RK])
        wdt = sb("wdt", [PARTS + RK, DI])
        alog = sb("alog", [P, KD * NS])
        wout = sb("wout", [P, KD, P])
        uvnat = sb("uvnat", [P, 2, NP, P])
        uvnat_pair = [sb(f"uvnat_pair{n}", [P, 2, NP, P], F32R) for n in range(2)]
        wp1 = sb("wp1", [P, P])
        wp2 = sb("wp2", [P, E])
        bp2r = sb("bp2r", [1, E])
        wo = sb("wo", [P, P])
        stats = sb("stats", [P, 2 * HB, 6])
        mv = sb("mv", [P, 2 * HB, 2])
        veps = sb("veps", [P, 2 * HB])
        rstd = sb("rstd", [P, 2 * HB])
        g1 = sb("g1", [P, HB])
        rt = sb("rt", [1, 6, HB, E])
        rs = sb("rs", [1, 6, HB])
        idx = sb("idx", [1, 2 * B], U32)
        w1s = sb("w1s", [P, 2, FH])
        w2s = sb("w2s", [P, 2, 2, P])
        b12s = sb("b12s", [P, B, 3])
        gf = sb("gf", [P, 2, 2, S])
        rT = sb("rT", [P, 2 * S])
        negA = sb("negA", [P, KD * NS])
        diagD = sb("diagD", [P, KD, P])
        bo3 = sb("bo3", [P, 1])
        with ExitStack() as scan_ctx:
            def early(name, shape, dt=F32):
                return scan_ctx.enter_context(nc.sbuf_tensor(name, shape, dt))

            xs = early("xs", [P, KD, HT])
            zs = early("zs", [P, KD, HT])
            eb = early("eb", [P, KD, HT])
            lnb = early("lnb", [P, KD, HT])
            delta = early("delta", [P, KD, HT])
            u = early("u", [P, KD, HT])
            poly = early("poly", [P, 2, HT])
            small = early("small", [P, HT], U8)
            bcf = early("bcf", [PARTS + RK, HT])
            res = early("res", [PARTS, HT])
            parts = early("parts", [PARTS, HT], BF16)
            mid = early("mid", [PARTS, HT], BF16)
            dA = early("dA", [P, 2, HB, S])
            dBu = early("dBu", [P, 2, HT])
            h = early("h", [P, 2, HT])
            hC = early("hC", [P, 2, HT])
            Csb = early("Csb", [P, 2, HT])
            yT = eb
        uvfT = [sb(f"uvfT{n}", [P, 2, CR], F32R) for n in range(2)]
        hT_pair = [sb(f"hT_pair{n}", [P, B * S], F32R) for n in range(2)]
        uvT_pair = [sb(f"uvT_pair{n}", [P, 2, 2 * S], F32R) for n in range(2)]
        v12T_pair = [sb(f"v12T_pair{n}", [P, 2, 2 * S], F32R) for n in range(2)]
        uvT = sb("uvT", [P, 2, 2 * S])
        nat = sb("nat", [P, 2, 4, P])
        tau = sb("tau", [P, 2, SB * S])
        qh = sb("qh", [P, 2, 2, SB, S])
        qhT = sb("qhT", [P, 2, SB, S])

        ld_x = [sem(f"ld_x{i}") for i in range(2)]
        ld_rows, ld_mamba, ld_late, ld_nat, ld_scan = (
            sem("ld_rows"), sem("ld_mamba"), sem("ld_late"), sem("ld_nat"), sem("ld_scan"))
        k_pool, k_dve, k_rows, k_cols, k_b12, k_b12c = (
            sem("k_pool"), sem("k_dve"), sem("k_rows"), sem("k_cols"), sem("k_b12"), sem("k_b12c"))
        k_expA, k_nat, k_natlow, k_uvf, k_uvfT, k_split, k_hTlow = (
            sem("k_expA"), sem("k_nat"), sem("k_natlow"), sem("k_uvf"), sem("k_uvfT"), sem("k_split"), sem("k_hTlow"))
        m_poly, m_polypool, m_partspool = sem("m_poly"), sem("m_polypool"), sem("m_partspool")
        fin_g, fin_gT, fin_xp, fin_x = sem("fin_g"), sem("fin_gT"), sem("fin_xp"), sem("fin_x")
        ln_stat, ln_mv, ln_eps, ln_rstd, ln_h, ln_xh, ln_tp, ln_hT = (
            sem("ln_stat"), sem("ln_mv"), sem("ln_eps"), sem("ln_rstd"), sem("ln_h"), sem("ln_xh"),
            sem("ln_tp"), sem("ln_hT"))
        rt_r1, rt_g, rt_r2, rt_d, rt_pow, rt_idx, rt_chain = (
            sem("rt_r1"), sem("rt_g"), sem("rt_r2"), sem("rt_d"), sem("rt_pow"), sem("rt_idx"),
            sem("rt_chain"))
        m_inp, m_silu, m_xp, m_bcf, m_parts, m_chain, m_dt, m_abs, m_e, m_ln, m_rel, m_u, m_y = (
            sem("m_inp"), sem("m_silu"), sem("m_xp"), sem("m_bcf"), sem("m_parts"), sem("m_chain"),
            sem("m_dt"), sem("m_abs"), sem("m_e"), sem("m_ln"), sem("m_rel"), sem("m_u"), sem("m_y"))
        s_B = [sem(f"s_B{r}") for r in range(2)]
        s_C = [sem(f"s_C{r}") for r in range(2)]
        s_Csb = [sem(f"s_Csb{r}") for r in range(2)]
        s_uB = [[sem(f"s_uB{r}{k}") for k in range(2)] for r in range(2)]
        s_dA = [[sem(f"s_dA{r}{k}") for k in range(2)] for r in range(2)]
        s_scan = [[sem(f"s_scan{r}{k}") for k in range(2)] for r in range(2)]
        s_hC = [[sem(f"s_hC{r}{k}") for k in range(2)] for r in range(2)]
        s_sum = [[sem(f"s_sum{r}{k}") for k in range(2)] for r in range(2)]
        w1_ld = [sem(f"w1_ld{s}") for s in range(2)]
        w2_ld = [sem(f"w2_ld{s}") for s in range(2)]
        f_h, f_g, f_r, f_rT = sem("f_h"), sem("f_g"), sem("f_r"), sem("f_rT")
        a_pr = [sem(f"a_pr{r}") for r in range(2)]
        a_uvh = [sem(f"a_uvh{r}") for r in range(2)]
        a_uv = [sem(f"a_uv{r}") for r in range(2)]
        a_uvT = [sem(f"a_uvT{r}") for r in range(2)]
        a_nt = [sem(f"a_nt{r}") for r in range(2)]
        a_nat = [sem(f"a_nat{r}") for r in range(2)]
        a_f = [sem(f"a_f{r}") for r in range(2)]
        a_tau = [[sem(f"a_tau{r}{i}") for i in range(2)] for r in range(2)]
        a_qh = [[sem(f"a_qh{r}{i}") for i in range(2)] for r in range(2)]
        a_t = [sem(f"a_t{r}") for r in range(2)]
        a_qhT = [sem(f"a_qhT{r}") for r in range(2)]
        a_pv = [sem(f"a_pv{r}") for r in range(2)]
        a_v12h = [sem(f"a_v12h{r}") for r in range(2)]
        a_v12 = [sem(f"a_v12{r}") for r in range(2)]
        a_g = [sem(f"a_g{r}") for r in range(2)]
        pool_passed, dve_passed = sem("pool_passed"), sem("dve_passed")
        st_out = sem("st_out")

        xv = x[:].rearrange("p (b k d) -> p b k d", b=B, k=SB)
        x_dram = x_in.rearrange("b (k p) d -> p b k d", p=P)
        out_dram = out.rearrange("b (k p) d -> p b k d", p=P)
        hTv = hT[:].rearrange("p (b s) -> p b s", s=S)

        LN_A0, LN_A1, LN_F1, LN_AT = 0, 2, 4, 8
        FIN_A, FIN_F1, FIN_AT, FIN_F2 = 0, 2, 6, 14
        RT_A, RT_AT = 0, 2
        XH_A, XH_AT = 0, 2

        block = ctx.enter_context(nc.Block())

        def runtime(v):
            return not isinstance(v, int)

        def at(v, scale, n):
            return bass.ds(v * scale, n) if runtime(v) else slice(v * scale, v * scale + n)

        def prev_batch(b):
            return bass.ds(b * S - S, S) if runtime(b) else slice((b - 1) * S, b * S)

        snapped = {}

        def prepare(eng, b):
            snapped[eng.engine] = {c: eng.snap(4 * b + c) for c in range(6)} if runtime(b) else None

        def cnt(eng, b, p):
            c = p // 2 + 1
            return snapped[eng.engine][c] if runtime(b) else 4 * b + c

        @block.sync
        def _(sp):
            for g in range(2):
                sp.dma_start(xv[:, g * HB:(g + 1) * HB], x_dram[:, g * HB:(g + 1) * HB]).then_inc(ld_x[g], 16)
                if g == 0:
                    sp.dma_start(win[:], Win).then_inc(ld_mamba, 16)
            wx_v = Wx.rearrange("(k p) n -> p k n", p=P)
            for i in range(3):
                sp.dma_start(wx[:, :, i * NBC:(i + 1) * NBC], wx_v[:, :, RK:]).then_inc(ld_mamba, 16)
            sp.dma_start(wx[:, :, PARTS:], wx_v[:, :, 0:RK]).then_inc(ld_mamba, 16)
            sp.dma_start(wdt[PARTS:PARTS + RK, :], Wdt).then_inc(ld_mamba, 16)
            sp.dma_start(wout[:], Wout.rearrange("(k p) n -> p k n", p=P)).then_inc(ld_late, 16)
            sp.dma_start(wp1[:], Wp1).then_inc(ld_late, 16)
            sp.dma_start(wp2[:], Wp2).then_inc(ld_late, 16)
            sp.dma_start(bp2r[:], bp2.rearrange("(a e) -> a e", a=1)).then_inc(ld_late, 16)
            sp.dma_start(wo[:], Wo).then_inc(ld_late, 16)
            sp.dma_start(uvnat[:, 0], Uf.rearrange("(c p) d -> p c d", p=P)).then_inc(ld_nat, 16)
            sp.dma_start(uvnat[:, 1], Vf.rearrange("(c p) d -> p c d", p=P)).then_inc(ld_nat, 16)

            def load_expert(f, i):
                j = 4 * f + i
                chosen = []
                for s in range(2):
                    wait(sp, rt_idx, (RT_A + 2 if runtime(i) or i >= 2 else RT_A + 1) if f == 0 else RT_AT + 2 * i + s + 1)
                    chosen.append(sp.value_load(idx[0:1, at(2 * i + (f * B + s), 1, 1)], min_val=0, max_val=E - 1))
                for s in range(2):
                    e = chosen[s]
                    wait(sp, f_h, 2 * j - 1 + s)
                    sp.dma_start(w1s[:, s, :], W1[bass.ds(e, 1), :, :].rearrange("a p n -> p (a n)")).then_inc(w1_ld[s], 16)
                    sp.dma_start(b12s[:, at(2 * i + s, 1, 1), :], b12all[:, bass.ds(e, 1), :]).then_inc(w1_ld[s], 16)
                for s in range(2):
                    wait(sp, f_r, 2 * j - 1 + s)
                    sp.dma_start(w2s[:, s, :, :], W2[bass.ds(chosen[s], 1), :, :].rearrange("a (c p) n -> p (a c) n", p=P))\
                        .then_inc(w2_ld[s], 16)

            sp.wait_ge(k_b12c, 1)
            load_expert(0, 0)
            with sp.Fori(1, 4) as i:
                load_expert(0, i)
            load_expert(1, 0)
            with sp.Fori(1, 4) as i:
                load_expert(1, i)
                sp.wait_ge(fin_x, FIN_F2 + i)
                sp.dma_start(out_dram[:, bass.ds(2 * i - 2, 2)], xv[:, bass.ds(2 * i - 2, 2)]).then_inc(st_out, 16)
            sp.wait_ge(fin_x, FIN_F2 + 4)
            sp.dma_start(out_dram[:, B - 2:B], xv[:, B - 2:B]).then_inc(st_out, 16)
            sp.wait_ge(st_out, 16 * 4)

        @block.gpsimd
        def _(pool):
            def copy(dst, src):
                return pool.tensor_scalar(dst, src, 1.0, 0.0, ALU.mult, ALU.add)

            k = Chain(pool, k_pool, 0)
            k(pool.memset(ident[:], 0.0))
            k(pool.affine_select(out=ident[:], in_=ident[:], compare_op=ALU.not_equal, fill=1.0, base=0,
                                 pattern=[[-1, P]], channel_multiplier=1))
            k(pool.memset(sel32[:], 0.0))
            for i in range(3):
                k(pool.affine_select(out=sel32[:], in_=sel32[:], compare_op=ALU.not_equal, fill=1.0,
                                     base=-NBC * i, pattern=[[-1, NBC]], channel_multiplier=1))
            k(pool.memset(neghalf[:], -0.5))
            k(pool.memset(econst[:], E_CONST))
            k(pool.memset(eps[:], 1e-5))
            k(pool.iota(iota8[:], pattern=[[1, E]], base=E, channel_multiplier=0, allow_small_or_imprecise_dtypes=True))

            def ln_rstd_(c, nb):
                n = SB * nb
                pool.wait_ge(ln_mv, c + 1)
                pool.tensor_tensor(veps[:, 0:n], mv[:, 0:n, 1], eps[:, 0:n], ALU.add).then_inc(ln_eps, 1)
                pool.wait_ge(ln_eps, c + 1)
                pool.tensor_tensor(rstd[:, 0:n], veps[:, 0:n], neghalf[:, 0:n], ALU.pow).then_inc(ln_rstd, 1)

            def rt_exp(r, nb):
                pool.wait_ge(rt_d, r + 1)
                pool.tensor_tensor(rt[:, 2, 0:nb], econst[:, 0:nb * E].rearrange("a (b e) -> a b e", e=E),
                                   rt[:, 1, 0:nb], ALU.pow).then_inc(rt_pow, 1)

            for g in range(2):
                ln_rstd_(LN_A0 + g, HB)
            k(copy(sel[:], sel32[:].unsqueeze(2).to_broadcast([PARTS, NBC, P])))

            def split_weights():
                pool.wait_ge(ld_nat, 32)
                copy(uvnat_pair[0][:], uvnat[:]).then_inc(k_nat, 1)
                pool.wait_ge(k_nat, 1)
                pool.tensor_tensor(uvnat_pair[1][:], uvnat[:], uvnat_pair[0][:].bitcast(F32), ALU.subtract)\
                    .then_inc(k_natlow, 1)

            def split_stream(i):
                tok = slice(2 * i * S, (2 * i + 2) * S)
                pool.wait_ge(ln_hT, LN_F1 + i + 1)
                copy(hT_pair[0][:, tok], hT[:, tok]).then_inc(k_split, 1)
                pool.wait_ge(k_split, i + 1)
                pool.tensor_tensor(hT_pair[1][:, tok], hT[:, tok], hT_pair[0][:, tok].bitcast(F32), ALU.subtract)\
                    .then_inc(k_hTlow, 1)

            def front(g):
                k_ = Chain(pool, m_partspool, 4 * g)
                pool.wait_ge(m_bcf, 2 * g + 2)
                k_(copy(parts[:], bcf[0:PARTS, :]))
                k_(pool.tensor_tensor(res[:], bcf[0:PARTS, :], parts[:], ALU.subtract))
                k_(copy(mid[2 * NBC:PARTS, :], res[2 * NBC:PARTS, :]))
                k_(copy(parts[NBC:2 * NBC, :], res[NBC:2 * NBC, :]))
                pool.tensor_tensor(parts[2 * NBC:PARTS, :], res[2 * NBC:PARTS, :], mid[2 * NBC:PARTS, :], ALU.subtract)\
                    .then_inc(m_parts, 1)
                k_ = Chain(pool, m_polypool, 3 * g)
                pool.wait_ge(m_parts, g + 1)
                pool.wait_ge(m_e, 2 * g + 2)
                k_(pool.tensor_scalar(hC[:, 0], eb[:, 1], 1.0 / 3.0, -0.5, ALU.mult, ALU.add))
                k_(pool.tensor_tensor(hC[:, 1], hC[:, 0], eb[:, 1], ALU.mult))
                k_(pool.tensor_scalar(hC[:, 0], hC[:, 1], 1.0, 1.0, ALU.mult, ALU.add))
                pool.tensor_tensor(poly[:, 1], hC[:, 0], eb[:, 1], ALU.mult).then_inc(m_poly, 1)
                pool.wait_ge(m_poly, g + 1)

            def scan_step(J, r):
                for k in range(2):
                    pool.wait_ge(s_scan[r][k], J + 1)
                    if k == 0:
                        pool.wait_ge(s_Csb[r], J + 1)
                    wait(pool, s_sum[1 - r][k], J + r)
                    pool.tensor_tensor(hC[:, k], h[:, k], Csb[:, r], ALU.mult).then_inc(s_hC[r][k], 1)

            for g in range(2):
                J0 = g * NS // 2
                if g == 0:
                    split_weights()
                front(g)
                for r in range(2):
                    scan_step(J0, r)
                with pool.Fori(J0 + 1, J0 + NS // 2) as J:
                    for r in range(2):
                        scan_step(J, r)
                ln_rstd_(LN_A1 + g, HB)
                rt_exp(RT_A + g, HB)

            for i in range(4):
                ln_rstd_(LN_F1 + i, 2)
                if i:
                    split_stream(i - 1)
            split_stream(3)

            def qh_step(b, p):
                for i in range(2):
                    pool.wait_ge(a_tau[p % 2][i], cnt(pool, b, p))
                    wait(pool, a_pv[p % 2], cnt(pool, b, p - 2))
                    pool.sem_inc(pool_passed, 1)
                    pool.tensor_scalar(qh[:, p % 2, i].rearrange("p k s -> p (k s)"), tau[:, i], 0.5, 0.5,
                                       ALU.mult, ALU.add).then_inc(a_qh[p % 2][i], 1)

            def batch(b, first=False, last=False):
                prepare(pool, b)
                for p in range(NP):
                    if not (last and p == NP - 1):
                        qh_step(b, p + 1)
                    if not first and p == 1:
                        ln_rstd_(LN_AT - 1 + b, 1)
                    if not first and p == 5:
                        rt_exp(RT_AT - 1 + b, 1)

            qh_step(0, 0)
            batch(0, first=True)
            with pool.Fori(1, B - 1) as b:
                batch(b)
            batch(B - 1, last=True)
            ln_rstd_(LN_AT + B - 1, 1)
            rt_exp(RT_AT + B - 1, 1)

        @block.scalar
        def _(act):
            act.dma_start(rows[0:NIN, :], bin_.rearrange("(c p) -> c p", p=P)).then_inc(ld_rows, 16)
            act.dma_start(rows[CB_DT:CB_DT + KD, :], bdt.rearrange("(c p) -> c p", p=P)).then_inc(ld_rows, 16)
            act.dma_start(rows[CB_DP:CB_DP + KD, :], Dp.rearrange("(c p) -> c p", p=P)).then_inc(ld_rows, 16)
            act.dma_start(rows[CB_BOUT:CB_BOUT + 1, :], bout.rearrange("(c p) -> c p", p=P)).then_inc(ld_rows, 16)
            act.dma_start(rows[CB_BO:CB_BO + 1, :], bo.rearrange("(c p) -> c p", p=P)).then_inc(ld_rows, 16)
            act.dma_start(rows[CB_BP1:CB_BP1 + 1, :], bp1.rearrange("(c p) -> c p", p=P)).then_inc(ld_rows, 16)
            bxr = bx.rearrange("(a n) -> a n", a=1)
            for i in range(3):
                act.dma_start(rows[CB_BX:CB_BX + 1, i * NBC:(i + 1) * NBC], bxr[:, RK:]).then_inc(ld_rows, 16)
            act.dma_start(rows[CB_BX:CB_BX + 1, PARTS:PARTS + RK], bxr[:, 0:RK]).then_inc(ld_rows, 16)
            act.dma_start(rows[CB_BX:CB_BX + 1, PARTS + RK:P], bxr[:, 0:P - PARTS - RK]).then_inc(ld_rows, 16)
            act.dma_start(b12rows[:, 0:FH], b1).then_inc(ld_rows, 16)
            act.dma_start(b12rows[:, FH:], b2).then_inc(ld_rows, 16)
            act.dma_start(alog[:].rearrange("p (k n) -> p k n", k=KD), A_log.rearrange("(k p) n -> p k n", p=P))\
                .then_inc(ld_scan, 16)

            def ln_copy(c, nb, tok, src):
                act.wait_ge(ln_tp, c + 1)
                act.activation(hT[:, tok], src, ACT.Copy).then_inc(ln_hT, 1)

            def fin_copy(f, nb, src, bias, scale):
                wait(act, fin_xp, f)
                act.activation(gT[:, 0:nb * S], src, ACT.Identity, bias=bias, scale=scale).then_inc(fin_gT, 1)

            def rt_gelu(r, nb, src):
                act.wait_ge(rt_r1, r + 1)
                act.activation(g1[:, 0:nb], src, ACT.Gelu, bias=cols[:, CB_BP1:CB_BP1 + 1]).then_inc(rt_g, 1)

            act.wait_ge(k_rows, 1)
            act.copy(cols[:], bank(7, ROWS)).then_inc(k_cols, 1)
            act.wait_ge(k_b12, 1)
            act.copy(b12all[:].rearrange("p e c -> p c e"), bank(6, 3 * E).rearrange("p (c e) -> p c e", e=E))\
                .then_inc(k_b12c, 1)
            act.wait_ge(ld_scan, 16)
            act.activation(negA[:], alog[:], ACT.Exp).then_inc(k_expA, 1)
            for g in range(2):
                ln_copy(LN_A0 + g, HB, slice(g * HT, (g + 1) * HT), ps[:, 4 * g * 512:4 * g * 512 + HT])
            act.wait_ge(k_cols, 1)

            def scan_step(J, r, j, first=False):
                for k in range(2):
                    if first:
                        act.wait_ge(m_u, 2 * g + k + 1)
                    wait(act, s_scan[1 - r][k], J + r)
                    n = k * NS + r + 2 * j
                    act.activation(dA[:, k, :, 1:], delta[:, k].rearrange("p (b s) -> p b s", s=S)[:, :, 1:],
                                   ACT.Exp, scale=negA[:, at(n, 1, 1)]).then_inc(s_dA[r][k], 1)
                act.wait_ge(s_C[r], J + 1)
                wait(act, s_hC[r][1], J)
                act.copy(Csb[:, r], ps[:, 2 * 512:2 * 512 + HT]).then_inc(s_Csb[r], 1)

            for g in range(2):
                for t in range(2 * NIN):
                    mc, nb = (t % 2) + 2 * (t // 4), (t // 2) % 2
                    dst = (xs if mc < KD else zs)[:, mc % KD, nb * 512:(nb + 1) * 512]
                    act.wait_ge(m_inp, 8 * g + t + 1)
                    act.activation(dst, bank(t % 4), ACT.Silu, bias=cols[:, CB_BIN + mc:CB_BIN + mc + 1])\
                        .then_inc(m_silu, 1)
                act.preload_act_table_set("natural_log_exp_and_others")
                for k in range(KD):
                    act.wait_ge(m_dt, 2 * g + k + 1)
                    act.activation(eb[:, k], ps[:, (4 + 2 * k) * 512:(6 + 2 * k) * 512], ACT.Abs,
                                   bias=cols[:, CB_DT + k:CB_DT + k + 1]).then_inc(m_abs, 1)
                for k in range(KD):
                    act.wait_ge(m_abs, 2 * g + k + 1)
                    act.activation(eb[:, k], eb[:, k], ACT.Exp, scale=-1.0).then_inc(m_e, 1)
                for k in range(KD):
                    act.wait_ge(m_e, 2 * g + k + 1)
                    act.activation(lnb[:, k], eb[:, k], ACT.Ln, bias=1.0).then_inc(m_ln, 1)
                J0 = g * NS // 2
                for r in range(2):
                    scan_step(J0, r, 0, first=True)
                with act.Fori(1, NS // 2) as j:
                    for r in range(2):
                        scan_step(j + J0, r, j)
                act.wait_ge(fin_g, FIN_A + g + 1)
                fin_copy(FIN_A + g, HB, ps[:, 0:HT], cols[:, CB_BOUT:CB_BOUT + 1], 1.0)
                ln_copy(LN_A1 + g, HB, slice(g * HT, (g + 1) * HT), ps[:, 0:HT])
                rt_gelu(RT_A + g, HB, bank(2, HB))

            for i in range(8):
                low, w, c = i // 4, i // 2 % 2, i % 2
                act.wait_ge(k_uvf, i + 1)
                act.copy(uvfT[low][:, w, c * 512:(c + 1) * 512], bank(4 + i % 4)).then_inc(k_uvfT, 1)

            def ffn_gelu(f, i):
                j = 4 * f + i
                for s in range(2):
                    wait(act, f_r, 2 * j - 1 + s)
                    act.wait_ge(f_h, 2 * j + s + 1)
                    for c in range(2):
                        ins = act.activation(gf[:, s, c], bank(s, S, c * S), ACT.Gelu,
                                             bias=b12s[:, at(2 * i + s, 1, 1), c])
                    ins.then_inc(f_g, 1)

            def ffn_fin(f, fi):
                act.wait_ge(fin_g, fi - (B if f else 0) + 1)
                fin_copy(fi, 2, bank(3), bo3[:, 0:1], 0.3)

            ffn_gelu(0, 0)
            with act.Fori(1, 4) as i:
                ffn_fin(0, FIN_F1 + i - 1)
                ffn_gelu(0, i)
                ln_copy(LN_F1 + i - 1, 2, bass.ds(i * 2 * S - 2 * S, 2 * S), bank(7))
            ffn_fin(0, FIN_F1 + 3)

            def tanh_step(b, p):
                for i in range(2):
                    act.wait_ge(a_f[p % 2], cnt(act, b, p))
                    wait(act, a_qh[(p - 1) % 2][i], cnt(act, b, p - 1))
                    act.activation(tau[:, i], bank(i), ACT.Tanh, scale=0.5).then_inc(a_tau[p % 2][i], 1)

            def uvT_step(b, p):
                act.wait_ge(a_uv[p % 2], cnt(act, b, p))
                wait(act, a_nt[p % 2], cnt(act, b, p - 2))
                act.mul(uvT[:, p % 2], bank(5), SCALE).then_inc(a_uvT[p % 2], 1)

            def nat_step(b, p):
                act.wait_ge(a_nt[p % 2], cnt(act, b, p))
                wait(act, a_pv[p % 2], cnt(act, b, p - 2))
                act.copy(nat[:, p % 2].rearrange("p a c -> p (a c)"), bank(6)).then_inc(a_nat[p % 2], 1)

            def batch(b, first=False, last=False):
                prepare(act, b)
                for p in range(NP):
                    if not (last and p == NP - 1):
                        tanh_step(b, p + 1)
                    if not (last and p >= NP - 2):
                        uvT_step(b, p + 2)
                    if not first:
                        if p == 3:
                            ln_copy(LN_AT - 1 + b, 1, prev_batch(b), bank(6, S))
                        if p == 4:
                            rt_gelu(RT_AT - 1 + b, 1, bank(6, 1))
                    if not (last and p == NP - 1):
                        nat_step(b, p + 1)
                    if not first and p == 0:
                        act.wait_ge(a_g[1], cnt(act, b, -1))
                        fin_copy(FIN_AT - 1 + b, 1, bank(7, S), 0.0, SCALE)

            uvT_step(0, 0)
            ln_copy(LN_F1 + 3, 2, slice(6 * S, 8 * S), bank(7))
            uvT_step(0, 1)
            tanh_step(0, 0)
            nat_step(0, 0)
            batch(0, first=True)
            with act.Fori(1, B - 1) as b:
                batch(b)
            batch(B - 1, last=True)
            act.wait_ge(a_g[1], cnt(act, B, -1))
            fin_copy(FIN_AT + B - 1, 1, bank(7, S), 0.0, SCALE)
            ln_copy(LN_AT + B - 1, 1, slice((B - 1) * S, B * S), bank(5, S))
            rt_gelu(RT_AT + B - 1, 1, bank(5, 1))

            ffn_gelu(1, 0)
            with act.Fori(1, 4) as i:
                ffn_fin(1, FIN_F2 + i - 1)
                ffn_gelu(1, i)
            ffn_fin(1, FIN_F2 + 3)

        @block.tensor
        def _(pe):
            def turn(dst, src, n=P):
                return pe.transpose(dst, src, ident[0:n, 0:n])

            def ln_turn(c, nb, dst):
                pe.wait_ge(ln_h, c + 1)
                for i in range(SB * nb):
                    ins = turn(dst[:, i * P:(i + 1) * P], hs[:, i * P:(i + 1) * P])
                ins.then_inc(ln_tp, 1)

            def fin_turn(f, nb, dst):
                pe.wait_ge(fin_gT, f + 1)
                for i in range(SB * nb):
                    ins = turn(dst[:, i * P:(i + 1) * P], gT[:, i * P:(i + 1) * P])
                ins.then_inc(fin_xp, 1)

            def rt_first(c, r, nb, b, dst):
                pe.wait_ge(ln_hT, c + 1)
                last = hTv[:, at(b, 1, nb), S - 1] if runtime(b) or nb == 1 else hTv[:, b:b + nb, S - 1]
                pe.matmul(dst[:, 0:nb], wp1[:], last, start=True, stop=True).then_inc(rt_r1, 1)

            def rt_second(r, nb, dst):
                pe.wait_ge(rt_g, r + 1)
                for i in range(nb):
                    ins = pe.matmul(dst[0:1, 64 + i * E:64 + (i + 1) * E], g1[:, i:i + 1], wp2[:], start=True, stop=True)
                ins.then_inc(rt_r2, 1)

            pe.wait_ge(k_pool, 2)
            pe.wait_ge(ld_rows, 16 * 13)
            turn(bank(7, ROWS), rows[:], ROWS).then_inc(k_rows, 1)
            for c in range(3):
                ins = turn(bank(6, E, c * E), b12rows[:, c * P:(c + 1) * P], E)
            ins.then_inc(k_b12, 1)
            for g in range(2):
                ln_turn(LN_A0 + g, HB, ps[:, 4 * g * 512:4 * g * 512 + HT])
            pe.wait_ge(ld_mamba, 16 * 6)

            def bcast(J, r, j, which):
                if which == 0:
                    wait(pe, s_uB[1 - r][1], J + r)
                else:
                    wait(pe, s_Csb[1 - r], J + r)
                row = which * NS + r + 2 * j
                for nb in range(NBK):
                    ins = pe.matmul(bank(2 * which + nb), sel[:, at(row, 1, 1), :].rearrange("q a m -> q (a m)"),
                                    parts[:, nb * 512:(nb + 1) * 512], start=True, stop=True)
                ins.then_inc((s_B if which == 0 else s_C)[r], 1)

            def add_up(J, r, stop=False):
                for k in range(2):
                    pe.wait_ge(s_hC[r][k], J + 1)
                    for nb in range(NBK):
                        ins = pe.matmul(bank(4 + 2 * k + nb), ident[:], hC[:, k, nb * 512:(nb + 1) * 512],
                                        start=False, stop=stop)
                    ins.then_inc(s_sum[r][k], 1)

            for g in range(2):
                pe.wait_ge(ln_hT, LN_A0 + 1 if g == 0 else LN_A1 + 1)
                if g:
                    pe.wait_ge(rt_d, RT_A + g)
                for t in range(2 * NIN):
                    mc, nb = (t % 2) + 2 * (t // 4), (t // 2) % 2
                    if t >= 4:
                        pe.wait_ge(m_silu, 8 * g + t - 3)
                    if t == 4 and g == 0:
                        pe.wait_ge(ln_hT, LN_A0 + 2)
                    pe.matmul(bank(t % 4), win[:, mc * P:(mc + 1) * P], hT[:, g * HT + nb * 512:g * HT + (nb + 1) * 512],
                              start=True, stop=True).then_inc(m_inp, 1)
                    if t in (4, 5):
                        nb = t - 4
                        pe.wait_ge(m_silu, 8 * g + 2 * nb + 2)
                        for k in range(KD):
                            ins = pe.matmul(ps[0:PARTS + RK, (4 + nb) * 512:(5 + nb) * 512], wx[:, k, :],
                                            xs[:, k, nb * 512:(nb + 1) * 512], start=(k == 0), stop=(k == KD - 1))
                        ins.then_inc(m_xp, 1)
                for k in range(KD):
                    for nb in range(NBK):
                        pe.wait_ge(m_bcf, 2 * g + NBK)
                        ins = pe.matmul(bank(4 + 2 * k + nb), wdt[PARTS:PARTS + RK, k * P:(k + 1) * P],
                                        bcf[PARTS:PARTS + RK, nb * 512:(nb + 1) * 512], start=True, stop=True)
                    ins.then_inc(m_dt, 1)
                pe.wait_ge(m_parts, g + 1)
                J0 = g * NS // 2
                pe.wait_ge(m_silu, 8 * g + 8)
                pe.wait_ge(k_pool, 11)
                for which in range(2):
                    bcast(J0, 0, 0, which)
                pe.wait_ge(k_dve, 3)
                for k in range(KD):
                    pe.wait_ge(m_abs, 2 * g + k + 1)
                    pe.wait_ge(m_rel, 2 * g + k + 1)
                    for nb in range(NBK):
                        pe.matmul(bank(4 + 2 * k + nb), diagD[:, k, :], xs[:, k, nb * 512:(nb + 1) * 512],
                                  start=True, stop=False)
                for which in range(2):
                    bcast(J0, 1, 0, which)
                add_up(J0, 0)
                with pe.Fori(1, NS // 2) as j:
                    J = pe.snap(j + J0)
                    for which in range(2):
                        bcast(J, 0, j, which)
                    add_up(J - 1, 1)
                    for which in range(2):
                        bcast(J, 1, j, which)
                    add_up(J, 0)
                add_up(J0 + NS // 2 - 1, 1, stop=True)
                pe.wait_ge(ld_late, 16 * 5)
                for nb in range(NBK):
                    for k in range(KD):
                        pe.wait_ge(m_y, 2 * g + k + 1)
                        ins = pe.matmul(bank(nb), wout[:, k, :], yT[:, k, nb * 512:(nb + 1) * 512],
                                        start=(k == 0), stop=(k == KD - 1))
                ins.then_inc(fin_g, 1)
                fin_turn(FIN_A + g, HB, ps[:, 2 * 512:2 * 512 + HT])
                ln_turn(LN_A1 + g, HB, ps[:, 0:HT])
                rt_first(LN_A1 + g, RT_A + g, HB, g * HB, bank(2))
                rt_second(RT_A + g, HB, bank(2))

            pe.wait_ge(k_natlow, 1)
            for i in range(8):
                low, w, c = i // 4, i // 2 % 2, i % 2
                if low:
                    pe.wait_ge(k_uvfT, i - 3)
                for n in range(4):
                    ins = turn(bank(4 + i % 4, P, n * P), uvnat_pair[low][:, w, 4 * c + n, :].bitcast(F32))
                ins.then_inc(k_uvf, 1)
            pe.wait_ge(k_uvfT, 8)
            pe.wait_ge(rt_d, RT_A + 2)

            def ffn_hidden(f, i):
                j = 4 * f + i
                for s in range(2):
                    pe.wait_ge(w1_ld[s], 32 * j + 32)
                    wait(pe, f_g, 2 * j - 1 + s)
                    for c in range(2):
                        ins = pe.matmul(bank(s, S, c * S), w1s[:, s, c * P:(c + 1) * P],
                                        hT[:, bass.ds(i * 2 * S + s * S, S) if runtime(i) else slice((2 * i + s) * S, (2 * i + s + 1) * S)],
                                        start=True, stop=True)
                    ins.then_inc(f_h, 1)

            def ffn_second(f, i):
                j = 4 * f + i
                for s in range(2):
                    pe.wait_ge(w2_ld[s], 16 * j + 16)
                    wait(pe, f_rT, 2 * j - 1 + s)
                    pe.wait_ge(f_g, 2 * j + s + 1)
                    for c in range(2):
                        ins = pe.matmul(bank(2 + 3 * s, S), w2s[:, s, c, :], gf[:, s, c], start=(c == 0), stop=(c == 1))
                    ins.then_inc(f_r, 1)

            def ffn_out(f, i):
                pe.wait_ge(f_rT, 2 * (4 * f + i) + 2)
                pe.matmul(bank(3), wo[:], rT[:], start=True, stop=True).then_inc(fin_g, 1)

            ffn_hidden(0, 0)
            ffn_second(0, 0)
            ffn_out(0, 0)
            with pe.Fori(1, 4) as i:
                ffn_hidden(0, i)
                fin_turn(FIN_F1 - 1 + i, 2, bank(4))
                ffn_second(0, i)
                ln_turn(LN_F1 - 1 + i, 2, bank(7))
                ffn_out(0, i)

            def split_matmul(dst, stationary, moving, start=True, stop=True):
                for n, (i, j) in enumerate(((0, 0), (0, 1), (1, 0))):
                    ins = pe.matmul(dst, stationary[i], moving[j], start=start and n == 0, stop=stop and n == 2)
                return ins

            def project(b, p):
                off = p // NP
                tok = bass.ds(b * S + off * S, S) if runtime(b) else slice((b + off) * S, (b + off + 1) * S)
                cols_p = slice((p % NP) * P, (p % NP + 1) * P)
                wait(pe, a_uvT[(p - 1) % 2], cnt(pe, b, p - 1))
                for w in range(2):
                    ins = split_matmul(bank(5, S, w * S), [a[:, w, cols_p] for a in uvfT],
                                       [a[:, tok] for a in hT_pair])
                ins.then_inc(a_pr[p % 2], 1)

            def messages(b, p):
                pe.wait_ge(a_uv[p % 2], cnt(pe, b, p))
                wait(pe, a_tau[(p - 1) % 2][1], cnt(pe, b, p - 1))
                for k in range(SB):
                    for i in range(2):
                        head = [uvT_pair[n][i * R:(i + 1) * R, p % 2] for n in range(2)]
                        ins = split_matmul(bank(i, S, k * S), [a[:, k * P:(k + 1) * P] for a in head],
                                           [a[:, S:2 * S] for a in head])
                ins.then_inc(a_f[p % 2], 1)

            def turn_uv(b, p):
                pe.wait_ge(a_uvT[p % 2], cnt(pe, b, p))
                wait(pe, a_nat[(p - 1) % 2], cnt(pe, b, p - 1))
                for i in range(4):
                    ins = turn(bank(6, P, i * P), uvT[:, p % 2, i * P:(i + 1) * P])
                ins.then_inc(a_nt[p % 2], 1)

            def turn_qh(b, p):
                wait(pe, a_qhT[(p - 1) % 2], cnt(pe, b, p - 1))
                for i in range(2):
                    pe.wait_ge(a_qh[p % 2][i], cnt(pe, b, p))
                    for k in range(SB):
                        for t in range(SB):
                            ins = turn(bank(2 + i, P, t * S + k * P), qh[:, p % 2, i, k, t * P:(t + 1) * P])
                ins.then_inc(a_t[p % 2], 1)

            def qhT_u(b, p):
                pe.wait_ge(a_nat[p % 2], cnt(pe, b, p))
                wait(pe, a_v12[(p - 1) % 2], cnt(pe, b, p - 1))
                for k in range(SB):
                    for i in range(2):
                        pe.matmul(ps[i * R:(i + 1) * R, 4 * 512 + S:5 * 512], nat[:, p % 2, k, i * R:(i + 1) * R],
                                  qh[:, p % 2, i, k, :], start=(k == 0), stop=(k == SB - 1))

            def qh_v(b, p):
                pe.wait_ge(a_qhT[p % 2], cnt(pe, b, p))
                for t in range(SB):
                    for i in range(2):
                        ins = pe.matmul(ps[i * R:(i + 1) * R, 4 * 512:4 * 512 + S], nat[:, p % 2, SB + t, i * R:(i + 1) * R],
                                        qhT[:, i, t, :], start=(t == 0), stop=(t == SB - 1))
                ins.then_inc(a_pv[p % 2], 1)

            def sum_pair(b, p):
                pe.wait_ge(a_v12[p % 2], cnt(pe, b, p))
                for w in range(2):
                    ins = split_matmul(bank(7, S), [a[:, w, p % NP, :] for a in uvnat_pair],
                                       [a[:, p % 2, w * S:(w + 1) * S] for a in v12T_pair],
                                       start=(p % NP == 0 and w == 0), stop=(p % NP == NP - 1 and w == 1))
                ins.then_inc(a_g[p % 2], 1)

            def batch(b, first=False, last=False):
                prepare(pe, b)
                for p in range(NP):
                    if not (last and p == NP - 1):
                        messages(b, p + 1)
                    if not (last and p >= NP - 2):
                        project(b, p + 2)
                    if not first and p in (1, 3, 4, 5):
                        pe.wait_ge(a_nat[p % 2], cnt(pe, b, p))
                        if p == 1:
                            fin_turn(FIN_AT - 1 + b, 1, bank(6, S))
                        if p == 3:
                            ln_turn(LN_AT - 1 + b, 1, bank(6, S))
                        if p == 4:
                            rt_first(LN_AT - 1 + b, RT_AT - 1 + b, 1, b - 1, bank(6))
                        if p == 5:
                            rt_second(RT_AT - 1 + b, 1, bank(6))
                    turn_qh(b, p)
                    qhT_u(b, p)
                    if not (first and p == 0):
                        sum_pair(b, p - 1)
                    qh_v(b, p)
                    if not first:
                        if p == 1:
                            pe.wait_ge(fin_x, FIN_AT + b)
                        if p == 3:
                            pe.wait_ge(ln_hT, LN_AT + b)
                        if p == 4:
                            pe.wait_ge(rt_g, RT_AT + b)
                        if p == 5:
                            pe.wait_ge(rt_d, RT_AT + b)
                    if not (last and p == NP - 1):
                        turn_uv(b, p + 1)

            fin_turn(FIN_F1 + 3, 2, bank(4))
            pe.wait_ge(k_hTlow, 1)
            project(0, 0)
            ln_turn(LN_F1 + 3, 2, bank(7))
            project(0, 1)
            messages(0, 0)
            turn_uv(0, 0)
            pe.wait_ge(ln_hT, LN_F1 + 4)
            pe.wait_ge(k_hTlow, 4)
            batch(0, first=True)
            with pe.Fori(1, B - 1) as b:
                batch(b)
            batch(B - 1, last=True)
            sum_pair(B - 1, NP - 1)
            fin_turn(FIN_AT + B - 1, 1, bank(5, S))
            pe.wait_ge(fin_x, FIN_AT + B)
            ln_turn(LN_AT + B - 1, 1, bank(5, S))
            rt_first(LN_AT + B - 1, RT_AT + B - 1, 1, B - 1, bank(5))
            rt_second(RT_AT + B - 1, 1, bank(5))
            pe.wait_ge(rt_d, RT_AT + B)

            ffn_hidden(1, 0)
            ffn_second(1, 0)
            ffn_out(1, 0)
            with pe.Fori(1, 4) as i:
                ffn_hidden(1, i)
                fin_turn(FIN_F2 - 1 + i, 2, bank(4))
                ffn_second(1, i)
                ffn_out(1, i)
            fin_turn(FIN_F2 + 3, 2, bank(4))

        @block.vector
        def _(dve):
            def ln_stats(c, nb, blk):
                for i in range(SB * nb):
                    ins = dve.bn_stats(stats[:, i, :], x[:, blk(i)])
                ins.then_inc(ln_stat, 1)
                wait(dve, ln_h, c)
                dve.wait_ge(ln_stat, c + 1)
                dve.sem_inc(dve_passed, 1)
                for i in range(SB * nb):
                    ins = dve.bn_aggr(mv[:, i, :], stats[:, i, :])
                ins.then_inc(ln_mv, 1)

            def ln_norm(c, nb, blk, xh=None):
                wait(dve, ln_tp, c)
                dve.wait_ge(ln_rstd, c + 1)
                for i in range(SB * nb):
                    ins = dve.tensor_scalar(hs[:, i * P:(i + 1) * P], x[:, blk(i)], mv[:, i, 0:1], rstd[:, i:i + 1],
                                            ALU.subtract, ALU.mult)
                ins.then_inc(ln_h, 1)
                if xh is not None:
                    dve.wait_ge(ln_h, c + 1)
                    whole = blk(0, SB * nb)
                    dve.tensor_tensor(x[:, whole], x[:, whole], hs[:, 0:SB * nb * P], ALU.add).then_inc(ln_xh, 1)

            def fin_add(f, nb, tok, src):
                dve.wait_ge(fin_xp, f + 1)
                dve.tensor_tensor(x[:, tok], src, x[:, tok], ALU.add).then_inc(fin_x, 1)
                dve.wait_ge(fin_x, f + 1)

            def rt_logits(r, nb, src):
                k = Chain(dve, rt_chain, r * RT_STEPS)
                dve.wait_ge(rt_r2, r + 1)
                k(dve.tensor_tensor(rt[:, 0, 0:nb], src[0:1, 64:64 + nb * E].rearrange("a (b e) -> a b e", e=E),
                                    bp2r[:].unsqueeze(1).to_broadcast([1, nb, E]), ALU.add))
                k(dve.tensor_reduce(rs[:, 0, 0:nb], rt[:, 0, 0:nb], AX, ALU.max))
                dve.tensor_tensor(rt[:, 1, 0:nb], rt[:, 0, 0:nb], rs[:, 0, 0:nb].unsqueeze(2).to_broadcast([1, nb, E]),
                                  ALU.subtract).then_inc(rt_d, 1)

            def rt_choose(r, nb, col):
                k = Chain(dve, rt_chain, r * RT_STEPS + 2)
                dve.wait_ge(rt_pow, r + 1)
                k(dve.tensor_reduce(rs[:, 1, 0:nb], rt[:, 2, 0:nb], AX, ALU.add))
                k(dve.reciprocal(rs[:, 2, 0:nb], rs[:, 1, 0:nb]))
                k(dve.tensor_tensor(rt[:, 3, 0:nb], rt[:, 2, 0:nb], rs[:, 2, 0:nb].unsqueeze(2).to_broadcast([1, nb, E]),
                                    ALU.mult))
                k(dve.tensor_reduce(rs[:, 3, 0:nb], rt[:, 3, 0:nb], AX, ALU.max))
                k(dve.tensor_tensor(rt[:, 4, 0:nb], rt[:, 3, 0:nb], rs[:, 3, 0:nb].unsqueeze(2).to_broadcast([1, nb, E]),
                                    ALU.is_ge))
                k(dve.tensor_scalar(rt[:, 4, 0:nb], rt[:, 4, 0:nb], -float(E), None, ALU.mult))
                k(dve.tensor_tensor(rt[:, 5, 0:nb], rt[:, 4, 0:nb], iota8[:].unsqueeze(1).to_broadcast([1, nb, E]), ALU.add))
                k(dve.tensor_reduce(rs[:, 4, 0:nb], rt[:, 5, 0:nb], AX, ALU.min))
                dve.tensor_copy(idx[:, col], rs[:, 4, 0:nb]).then_inc(rt_idx, 1)

            def blocks(start, scale=1):
                def blk(i, n=1):
                    if runtime(start):
                        return bass.ds(start * P + i * P, n * P)
                    return slice((start + i) * P, (start + i + n) * P)
                return blk

            dve.memset(dA[:, :, :, 0], 0.0).then_inc(k_dve, 1)
            for g in range(2):
                dve.wait_ge(ld_x[g], 16)
                ln_stats(LN_A0 + g, HB, blocks(g * 2 * HB))
                ln_norm(LN_A0 + g, HB, blocks(g * 2 * HB))
            dve.wait_ge(k_cols, 1)
            dve.wait_ge(k_pool, 10)
            dve.tensor_scalar(bo3[:], cols[:, CB_BO:CB_BO + 1], 0.3, None, ALU.mult).then_inc(k_dve, 1)
            for k in range(KD):
                ins = dve.tensor_scalar(diagD[:, k, :], ident[:], cols[:, CB_DP + k:CB_DP + k + 1], None, ALU.mult)
            ins.then_inc(k_dve, 1)
            dve.wait_ge(k_expA, 1)
            dve.tensor_scalar(negA[:], negA[:], -1.0, None, ALU.mult).then_inc(k_dve, 1)

            def scan_step(J, r):
                for k in range(2):
                    if k == 0:
                        dve.wait_ge(s_B[r], J + 1)
                    wait(dve, s_scan[1 - r][k], J + r)
                    dve.tensor_tensor(dBu[:, k], ps[:, 0:HT], u[:, k], ALU.mult).then_inc(s_uB[r][k], 1)
                    dve.wait_ge(s_dA[r][k], J + 1)
                    dve.wait_ge(s_uB[r][k], J + 1)
                    wait(dve, s_hC[1 - r][k], J + r)
                    dve.tensor_tensor_scan(h[:, k], dA[:, k].rearrange("p b s -> p (b s)"), dBu[:, k], 0.0,
                                           ALU.mult, ALU.add).then_inc(s_scan[r][k], 1)

            FRONT = 9
            for g in range(2):
                k_ = Chain(dve, m_chain, g * FRONT)
                for nb in range(NBK):
                    dve.wait_ge(m_xp, 2 * g + nb + 1)
                    dve.tensor_scalar(bcf[:, nb * 512:(nb + 1) * 512], ps[0:PARTS + RK, (4 + nb) * 512:(5 + nb) * 512],
                                      cols[0:PARTS + RK, CB_BX:CB_BX + 1], None, ALU.add).then_inc(m_bcf, 1)
                for k in range(KD):
                    dve.wait_ge(m_abs, 2 * g + k + 1)
                    dve.tensor_scalar(delta[:, k], ps[:, (4 + 2 * k) * 512:(6 + 2 * k) * 512],
                                      cols[:, CB_DT + k:CB_DT + k + 1], 0.0, ALU.add, ALU.max).then_inc(m_rel, 1)
                for k in range(KD):
                    dve.wait_ge(m_e, 2 * g + k + 1)
                    e = eb[:, k]
                    k_(dve.tensor_scalar(small[:], e, LOG1P_SPLIT, None, ALU.is_lt))
                    if k == 0:
                        k_(dve.tensor_scalar(dBu[:, 0], e, 1.0 / 3.0, -0.5, ALU.mult, ALU.add))
                        k_(dve.tensor_tensor(dBu[:, 1], dBu[:, 0], e, ALU.mult))
                        k_(dve.scalar_tensor_tensor(out=poly[:, 0], in0=dBu[:, 1], scalar=1.0, in1=e, op0=ALU.add,
                                                    op1=ALU.mult))
                    else:
                        dve.wait_ge(m_poly, g + 1)
                    dve.wait_ge(m_ln, 2 * g + k + 1)
                    k_(dve.copy_predicated(lnb[:, k], small[:], poly[:, k]))
                    k_(dve.tensor_tensor(delta[:, k], delta[:, k], lnb[:, k], ALU.add))
                    dve.tensor_tensor(u[:, k], delta[:, k], xs[:, k], ALU.mult).then_inc(m_u, 1)
                dve.wait_ge(m_u, 2 * g + 2)
                J0 = g * NS // 2
                for r in range(2):
                    scan_step(J0, r)
                with dve.Fori(J0 + 1, J0 + NS // 2) as J:
                    for r in range(2):
                        scan_step(J, r)
                for k in range(KD):
                    dve.wait_ge(s_sum[1][k], J0 + NS // 2)
                    dve.tensor_tensor(yT[:, k], ps[:, (4 + 2 * k) * 512:(6 + 2 * k) * 512], zs[:, k], ALU.mult)\
                        .then_inc(m_y, 1)
                fin_add(FIN_A + g, HB, slice(g * HT, (g + 1) * HT), ps[:, 2 * 512:2 * 512 + HT])
                ln_stats(LN_A1 + g, HB, blocks(g * 2 * HB))
                ln_norm(LN_A1 + g, HB, blocks(g * 2 * HB), xh=XH_A + g)
                if g == 0:
                    dve.wait_ge(ld_late, 16 * 5)
                rt_logits(RT_A + g, HB, bank(2))
                rt_choose(RT_A + g, HB, slice(g * HB, (g + 1) * HB))

            def ffn_bias(f, i):
                j = 4 * f + i
                for s in range(2):
                    if s == 0:
                        wait(dve, fin_g, 2 + j)
                    dve.wait_ge(f_r, 2 * j + s + 1)
                    dve.tensor_scalar(rT[:, s * S:(s + 1) * S], bank(2 + 3 * s, S), b12s[:, at(2 * i + s, 1, 1), 2],
                                      None, ALU.add).then_inc(f_rT, 1)

            ffn_bias(0, 0)
            dve.wait_ge(ln_xh, XH_A + 2)
            with dve.Fori(1, 4) as i:
                fin_add(FIN_F1 - 1 + i, 2, bass.ds(i * 2 * S - 2 * S, 2 * S), bank(4))
                ln_stats(LN_F1 - 1 + i, 2, blocks(i * 4 - 4))
                ffn_bias(0, i)
                ln_norm(LN_F1 - 1 + i, 2, blocks(i * 4 - 4))
            fin_add(FIN_F1 + 3, 2, slice(6 * S, 8 * S), bank(4))
            ln_stats(LN_F1 + 3, 2, blocks(12))

            def uv_step(b, p):
                wait(dve, a_f[p % 2], cnt(dve, b, p - 2))
                dve.wait_ge(a_pr[p % 2], cnt(dve, b, p))
                dve.tensor_scalar(uvT_pair[0][:, p % 2], bank(5), SCALE, None, ALU.mult).then_inc(a_uvh[p % 2], 1)
                dve.wait_ge(a_uvh[p % 2], cnt(dve, b, p))
                dve.scalar_tensor_tensor(out=uvT_pair[1][:, p % 2], in0=bank(5), scalar=SCALE,
                                         in1=uvT_pair[0][:, p % 2].bitcast(F32), op0=ALU.mult, op1=ALU.subtract)\
                    .then_inc(a_uv[p % 2], 1)

            def batch(b, first=False, last=False):
                prepare(dve, b)
                prev = blocks(b * 2 - 2)
                for p in range(NP):
                    if not (last and p >= NP - 2):
                        uv_step(b, p + 2)
                    if not first and p == 1:
                        fin_add(FIN_AT - 1 + b, 1, prev_batch(b), bank(6, S))
                    wait(dve, a_pv[(p - 1) % 2], cnt(dve, b, p - 1))
                    dve.wait_ge(a_t[p % 2], cnt(dve, b, p))
                    for i in range(2):
                        ins = dve.tensor_copy(qhT[:, i].rearrange("p k s -> p (k s)"), bank(2 + i))
                    ins.then_inc(a_qhT[p % 2], 1)
                    if not first:
                        if p == 1:
                            ln_stats(LN_AT - 1 + b, 1, prev)
                        if p == 2:
                            ln_norm(LN_AT - 1 + b, 1, prev, xh=True)
                        if p == 5:
                            rt_logits(RT_AT - 1 + b, 1, bank(6))
                        if p == 6:
                            rt_choose(RT_AT - 1 + b, 1, bass.ds(b + (B - 1), 1) if runtime(b) else slice(B + b - 1, B + b))
                    wait(dve, a_g[p % 2], cnt(dve, b, p - 2))
                    dve.wait_ge(a_pv[p % 2], cnt(dve, b, p))
                    dve.tensor_copy(v12T_pair[0][:, p % 2], bank(4)).then_inc(a_v12h[p % 2], 1)
                    dve.wait_ge(a_v12h[p % 2], cnt(dve, b, p))
                    dve.tensor_tensor(v12T_pair[1][:, p % 2], bank(4), v12T_pair[0][:, p % 2].bitcast(F32), ALU.subtract)\
                        .then_inc(a_v12[p % 2], 1)

            uv_step(0, 0)
            ln_norm(LN_F1 + 3, 2, blocks(12))
            uv_step(0, 1)
            batch(0, first=True)
            with dve.Fori(1, B - 1) as b:
                batch(b)
            batch(B - 1, last=True)
            fin_add(FIN_AT + B - 1, 1, slice((B - 1) * S, B * S), bank(5, S))
            ln_stats(LN_AT + B - 1, 1, blocks(2 * B - 2))
            ln_norm(LN_AT + B - 1, 1, blocks(2 * B - 2), xh=True)
            rt_logits(RT_AT + B - 1, 1, bank(5))
            rt_choose(RT_AT + B - 1, 1, slice(2 * B - 1, 2 * B))

            ffn_bias(1, 0)
            dve.wait_ge(ln_xh, XH_AT + B)
            with dve.Fori(1, 4) as i:
                fin_add(FIN_F2 - 1 + i, 2, bass.ds(i * 2 * S - 2 * S, 2 * S), bank(4))
                ffn_bias(1, i)
            fin_add(FIN_F2 + 3, 2, slice(6 * S, 8 * S), bank(4))


_INS = ['L0_attn_a_x', 'L0_attn_a_Win', 'L0_attn_a_bin', 'L0_attn_a_Wx', 'L0_attn_a_bx', 'L0_attn_a_Wdt',
        'L0_attn_a_bdt', 'L0_attn_a_A_log', 'L0_attn_a_Dp', 'L0_attn_a_Wout', 'L0_attn_a_bout',
        'L0_attn_b_ternary_factor_u', 'L0_attn_b_ternary_factor_v', 'L0_ffn_Wp1', 'L0_ffn_bp1', 'L0_ffn_Wp2',
        'L0_ffn_bp2', 'L0_ffn_W1', 'L0_ffn_b1', 'L0_ffn_W2', 'L0_ffn_b2', 'L0_ffn_Wo', 'L0_ffn_bo']


def kernel(**inputs):
    import numpy as np
    import concourse.bacc as bacc
    from concourse.bass_utils import run_bass_kernel_spmd

    nc = bacc.Bacc("TRN2", target_bir_lowering=False, num_devices=1)
    arrays, args = {}, []
    for name in _INS:
        a = np.ascontiguousarray(inputs[name])
        arrays[f"in_{name}"] = a
        args.append(nc.dram_tensor(f"in_{name}", a.shape, mybir.dt.from_np(a.dtype), kind="ExternalInput").ap())
    out = nc.dram_tensor("out_x", inputs['L0_attn_a_x'].shape, F32, kind="ExternalOutput").ap()
    build(nc, *args, out)
    result = run_bass_kernel_spmd(nc, [arrays], core_ids=[0])
    return result.results[0]["out_x"]
```

```python
from contextlib import ExitStack

import concourse.bass as bass
from concourse import mybir

F32 = mybir.dt.float32
BF16 = mybir.dt.bfloat16
F32R = mybir.dt.float32r
U32 = mybir.dt.uint32
U8 = mybir.dt.uint8
ALU = mybir.AluOpType
ACT = mybir.ActivationFunctionType
AX = mybir.AxisListType.X

P = 128
E_CONST = 2.718281828459045
LOG1P_SPLIT = 2.0 ** -7


def wait(eng, sem, value):
    if not isinstance(value, int) or value > 0:
        eng.wait_ge(sem, value)


class Chain:

    def __init__(self, eng, sem, base):
        self.eng, self.sem, self.count = eng, sem, base

    def __call__(self, instruction):
        self.count = self.count + 1
        instruction.then_inc(self.sem, 1)
        self.eng.wait_ge(self.sem, self.count)


def build(nc, x_in, Win, bin_, Wx, bx, Wdt, bdt, A_log, Dp, Wout, bout, Uf, Vf,
          Wp1, bp1, Wp2, bp2, W1, b1, W2, b2, Wo, bo, out):
    B, S, D = x_in.shape
    DI, NS = A_log.shape
    RK = Wdt.shape[0]
    KD = DI // P
    HB = B // 2
    HT = HB * S
    NBK = HT // 512
    CR = Uf.shape[0]
    NP = CR // P
    R = 64
    E, _, FH = W1.shape
    SB = S // P
    SCALE = 0.03125
    NIN = 2 * DI // P
    NBC = 2 * NS
    PARTS = 3 * NBC
    ROWS = NIN + 2 * KD + 4
    CB_BIN, CB_DT, CB_DP = 0, NIN, NIN + KD
    CB_BOUT, CB_BO, CB_BP1, CB_BX = ROWS - 4, ROWS - 3, ROWS - 2, ROWS - 1
    assert D == P and S == 256 and NP == 8 and KD == 2 and E == 8 and FH == 2 * P and NBK == 2
    RT_STEPS = 10

    with ExitStack() as ctx:
        def sb(name, shape, dt=F32):
            return ctx.enter_context(nc.sbuf_tensor(name, shape, dt))

        def sem(name):
            return ctx.enter_context(nc.semaphore(name))

        ps = ctx.enter_context(nc.psum_tensor("ps", [P, 8 * 512], F32))

        def bank(i, n=512, at=0):
            return ps[:, 512 * i + at:512 * i + at + n]

        x = sb("x", [P, B * S])
        hT = sb("hT", [P, B * S])
        hs = sb("hs", [P, 2 * HB * P])
        gT = sb("gT", [P, HT])
        ident = sb("ident", [P, P])
        sel32 = sb("sel32", [PARTS, NBC], BF16)
        sel = sb("sel", [PARTS, NBC, P], BF16)
        neghalf = sb("neghalf", [P, 2 * HB])
        econst = sb("econst", [B, E])
        iota8 = sb("iota8", [B, E])
        eps = sb("eps", [P, 2 * HB])
        rows = sb("rows", [ROWS, P])
        cols = sb("cols", [P, ROWS])
        b12rows = sb("b12rows", [E, 3 * P])
        b12all = sb("b12all", [P, E, 3])
        win = sb("win", [P, 2 * DI])
        wx = sb("wx", [P, KD, PARTS + RK])
        wdt = sb("wdt", [PARTS + RK, DI])
        alog = sb("alog", [P, KD * NS])
        wout = sb("wout", [P, KD, P])
        uvnat_pair = [sb(f"uvnat_pair{n}", [P, 2, NP, P], F32R) for n in range(2)]
        wp1 = sb("wp1", [P, P])
        wp2 = sb("wp2", [P, E])
        bp2r = sb("bp2r", [B, E])
        wo = sb("wo", [P, P])
        stats = sb("stats", [P, 2 * HB, 6])
        mv = sb("mv", [P, 2 * HB, 2])
        veps = sb("veps", [P, 2 * HB])
        rstd = sb("rstd", [P, 2 * HB])
        g1 = sb("g1", [P, B])
        rt = sb("rt", [B, 6, E])
        rs = sb("rs", [B, 6])
        idx = sb("idx", [1, 2 * B], U32)
        b12s = sb("b12s", [P, B, 3])
        negA = sb("negA", [P, KD * NS])
        diagD = sb("diagD", [P, KD, P])
        bo3 = sb("bo3", [P, 1])
        with ExitStack() as scan_ctx:
            def early(name, shape, dt=F32):
                return scan_ctx.enter_context(nc.sbuf_tensor(name, shape, dt))

            xs = early("xs", [P, 2, KD, HT])
            zs = early("zs", [P, 2, KD, HT])
            delta = early("delta", [P, 2, KD, HT])
            u = early("u", [P, 2, KD, HT])
            small = early("small", [P, HT], U8)
            parts = early("parts", [PARTS, 2, HT], BF16)
            mid = early("mid", [PARTS, HT], BF16)
            dA = early("dA", [P, 2, HB, S])
            dBu = early("dBu", [P, 2, KD, HT])
            h = early("h", [P, 2, KD, HT])
            hC = early("hC", [P, 2, HT])
            Csb = early("Csb", [P, 2, HT])
            yT = early("yT", [P, KD, HT])
        eb = (h[:, 0], dA[:].rearrange("p k b s -> p k (b s)"))
        poly = (hC[:], h[:, 1])
        lnb = (u[:, 0], u[:, 1])
        bcf = (Csb[0:PARTS + RK, 0], yT[0:PARTS + RK, 0])
        res = (Csb[0:PARTS, 1], yT[0:PARTS, 1])
        uvnat = yT[:].rearrange("p w (c d) -> p w c d", d=P)
        w1s = sb("w1s", [P, 4, FH])
        w2s = sb("w2s", [P, 4, 2, P])
        gf = sb("gf", [P, 2, 2, S])
        rT = sb("rT", [P, 2 * S])
        uvfT = [sb(f"uvfT{n}", [P, 2, CR], F32R) for n in range(2)]
        hT_pair = [sb(f"hT_pair{n}", [P, B * S], F32R) for n in range(2)]
        uvT_pair = [sb(f"uvT_pair{n}", [P, 2, 2 * S], F32R) for n in range(2)]
        v12T_pair = [sb(f"v12T_pair{n}", [P, 2, 2 * S], F32R) for n in range(2)]
        uvT = sb("uvT", [P, 2, 2 * S])
        nat = sb("nat", [P, 2, 4, P])
        tau = sb("tau", [P, 2, SB * S])
        qh = sb("qh", [P, 2, 2, SB, S])
        qhT = sb("qhT", [P, 2, SB, S])

        ld_x = [sem(f"ld_x{i}") for i in range(2)]
        ld_rows, ld_win, ld_mamba, ld_late, ld_nat, ld_scan = (
            sem("ld_rows"), sem("ld_win"), sem("ld_mamba"), sem("ld_late"), sem("ld_nat"), sem("ld_scan"))
        k_pool, k_dve, k_rows, k_cols, k_b12, k_b12c = (
            sem("k_pool"), sem("k_dve"), sem("k_rows"), sem("k_cols"), sem("k_b12"), sem("k_b12c"))
        k_expA, k_nat, k_natlow, k_uvf, k_uvfT, k_split, k_hTlow = (
            sem("k_expA"), sem("k_nat"), sem("k_natlow"), sem("k_uvf"), sem("k_uvfT"), sem("k_split"), sem("k_hTlow"))
        m_w, m_poly, m_polypool, m_partspool = sem("m_w"), sem("m_poly"), sem("m_polypool"), sem("m_partspool")
        fin_g, fin_gT, fin_xp, fin_x = sem("fin_g"), sem("fin_gT"), sem("fin_xp"), sem("fin_x")
        ln_stat, ln_mv, ln_eps, ln_rstd, ln_h, ln_xh, ln_tp, ln_hT = (
            sem("ln_stat"), sem("ln_mv"), sem("ln_eps"), sem("ln_rstd"), sem("ln_h"), sem("ln_xh"),
            sem("ln_tp"), sem("ln_hT"))
        rt_r1, rt_g, rt_r2, rt_d, rt_pow, rt_idx, rt_chain, rt_row = (
            sem("rt_r1"), sem("rt_g"), sem("rt_r2"), sem("rt_d"), sem("rt_pow"), sem("rt_idx"),
            sem("rt_chain"), sem("rt_row"))
        rt_turned = sem("rt_turned")
        m_inp, m_silu, m_xp, m_bcf, m_parts, m_chain, m_dt, m_abs, m_e, m_ln, m_rel, m_u, m_y = (
            sem("m_inp"), sem("m_silu"), sem("m_xp"), sem("m_bcf"), sem("m_parts"), sem("m_chain"),
            sem("m_dt"), sem("m_abs"), sem("m_e"), sem("m_ln"), sem("m_rel"), sem("m_u"), sem("m_y"))
        s_B = [sem(f"s_B{r}") for r in range(2)]
        s_C = [sem(f"s_C{r}") for r in range(2)]
        s_Csb = [sem(f"s_Csb{r}") for r in range(2)]
        s_uB = [[sem(f"s_uB{r}{k}") for k in range(2)] for r in range(2)]
        s_dA = [[sem(f"s_dA{r}{k}") for k in range(2)] for r in range(2)]
        s_scan = [[sem(f"s_scan{r}{k}") for k in range(2)] for r in range(2)]
        s_hC = [[sem(f"s_hC{r}{k}") for k in range(2)] for r in range(2)]
        s_sum = [[sem(f"s_sum{r}{k}") for k in range(2)] for r in range(2)]
        w1_ld = [sem(f"w1_ld{s}") for s in range(4)]
        w2_ld = [sem(f"w2_ld{s}") for s in range(4)]
        f_h, f_g, f_r, f_rT = sem("f_h"), sem("f_g"), sem("f_r"), sem("f_rT")
        a_pr = [sem(f"a_pr{r}") for r in range(2)]
        a_uvh = [sem(f"a_uvh{r}") for r in range(2)]
        a_uv = [sem(f"a_uv{r}") for r in range(2)]
        a_uvT = [sem(f"a_uvT{r}") for r in range(2)]
        a_nt = [sem(f"a_nt{r}") for r in range(2)]
        a_nat = [sem(f"a_nat{r}") for r in range(2)]
        a_f = [sem(f"a_f{r}") for r in range(2)]
        a_tau = [[sem(f"a_tau{r}{i}") for i in range(2)] for r in range(2)]
        a_qh = [[sem(f"a_qh{r}{i}") for i in range(2)] for r in range(2)]
        a_t = [[sem(f"a_t{r}{i}") for i in range(2)] for r in range(2)]
        a_qhT = [[sem(f"a_qhT{r}{i}") for i in range(2)] for r in range(2)]
        a_pv = [sem(f"a_pv{r}") for r in range(2)]
        a_v12h = [sem(f"a_v12h{r}") for r in range(2)]
        a_v12 = [sem(f"a_v12{r}") for r in range(2)]
        a_g = [sem(f"a_g{r}") for r in range(2)]
        pool_passed, dve_passed = sem("pool_passed"), sem("dve_passed")
        st_out, st_last = sem("st_out"), sem("st_last")

        xv = x[:].rearrange("p (b k d) -> p b k d", b=B, k=SB)
        x_dram = x_in.rearrange("b (k p) d -> p b k d", p=P)
        out_dram = out.rearrange("b (k p) d -> p b k d", p=P)
        hTv = hT[:].rearrange("p (b s) -> p b s", s=S)

        LN_A0, LN_A1, LN_F1, LN_AT = 0, 4, 6, 10
        FIN_A, FIN_F1, FIN_AT, FIN_F2 = 0, 2, 6, 14
        RT_A, RT_AT = 0, 2
        XH_A, XH_AT = 0, 2

        block = ctx.enter_context(nc.Block())

        def runtime(v):
            return not isinstance(v, int)

        def at(v, scale, n):
            return bass.ds(v * scale, n) if runtime(v) else slice(v * scale, v * scale + n)

        def prev_batch(b):
            return bass.ds(b * S - S, S) if runtime(b) else slice((b - 1) * S, b * S)

        snapped = {}

        def prepare(eng, b):
            snapped[eng.engine] = {c: eng.snap(4 * b + c) for c in range(6)} if runtime(b) else None

        def cnt(eng, b, p):
            c = p // 2 + 1
            return snapped[eng.engine][c] if runtime(b) else 4 * b + c

        def block_number(g, t):
            return 4 * g + t % 4 + (8 if t >= 4 else 0)

        @block.sync
        def _(sp):
            for g in range(2):
                sp.dma_start(xv[:, g * HB:(g + 1) * HB], x_dram[:, g * HB:(g + 1) * HB]).then_inc(ld_x[g], 16)
                if g == 0:
                    sp.dma_start(win[:], Win).then_inc(ld_win, 16)
            bxr = bx.rearrange("(a n) -> a n", a=1)
            for i in range(3):
                sp.dma_start(rows[CB_BX:CB_BX + 1, i * NBC:(i + 1) * NBC], bxr[:, RK:]).then_inc(ld_rows, 16)
            sp.dma_start(rows[CB_BX:CB_BX + 1, PARTS:PARTS + RK], bxr[:, 0:RK]).then_inc(ld_rows, 16)
            sp.dma_start(rows[CB_BX:CB_BX + 1, PARTS + RK:P], bxr[:, 0:P - PARTS - RK]).then_inc(ld_rows, 16)
            wx_v = Wx.rearrange("(k p) n -> p k n", p=P)
            for i in range(3):
                sp.dma_start(wx[:, :, i * NBC:(i + 1) * NBC], wx_v[:, :, RK:]).then_inc(ld_mamba, 16)
            sp.dma_start(wx[:, :, PARTS:], wx_v[:, :, 0:RK]).then_inc(ld_mamba, 16)
            sp.dma_start(wdt[PARTS:PARTS + RK, :], Wdt).then_inc(ld_mamba, 16)
            sp.dma_start(wout[:], Wout.rearrange("(k p) n -> p k n", p=P)).then_inc(ld_late, 16)
            sp.dma_start(wp1[:], Wp1).then_inc(ld_late, 16)
            sp.dma_start(wp2[:], Wp2).then_inc(ld_late, 16)
            sp.dma_start(bp2r[:], bp2.rearrange("(a e) -> a e", a=1).to_broadcast([B, E])).then_inc(ld_late, 16)
            sp.dma_start(wo[:], Wo).then_inc(ld_late, 16)
            sp.dma_start(uvnat[:, 0], Uf.rearrange("(c p) d -> p c d", p=P)).then_inc(ld_nat, 16)
            sp.dma_start(uvnat[:, 1], Vf.rearrange("(c p) d -> p c d", p=P)).then_inc(ld_nat, 16)

            def load_expert(f, i):
                j = 4 * f + i
                for group in ((0,), (1,)) if (f, i) == (1, 3) else ((0, 1),):
                    chosen = {}
                    for s in group:
                        sp.wait_ge(rt_idx, RT_A + i // 2 + 1 if f == 0 else RT_AT + 2 * i + s + 1)
                        chosen[s] = sp.value_load(idx[0:1, 2 * i + f * B + s:2 * i + f * B + s + 1], min_val=0, max_val=E - 1)
                    for s in group:
                        slot = 2 * (j % 2) + s
                        wait(sp, f_h, 2 * j - 3 + s)
                        sp.dma_start(w1s[:, slot, :], W1[bass.ds(chosen[s], 1), :, :].rearrange("a p n -> p (a n)"))\
                            .then_inc(w1_ld[slot], 16)
                        sp.dma_start(b12s[:, 2 * i + s:2 * i + s + 1, :], b12all[:, bass.ds(chosen[s], 1), :])\
                            .then_inc(w1_ld[slot], 16)
                    for s in group:
                        slot = 2 * (j % 2) + s
                        wait(sp, f_r, 2 * j - 3 + s)
                        sp.dma_start(w2s[:, slot, :, :],
                                     W2[bass.ds(chosen[s], 1), :, :].rearrange("a (c p) n -> p (a c) n", p=P))\
                            .then_inc(w2_ld[slot], 16)

            sp.wait_ge(k_b12c, 1)
            for f in range(2):
                for i in range(4):
                    load_expert(f, i)
            sp.wait_ge(fin_x, FIN_F2 + 4)
            sp.dma_start(out_dram[:, B - 2:B], xv[:, B - 2:B]).then_inc(st_last, 16)
            sp.wait_ge(st_out, 16 * 3)
            sp.wait_ge(st_last, 16)

        @block.gpsimd
        def _(pool):
            def copy(dst, src):
                return pool.tensor_scalar(dst, src, 1.0, 0.0, ALU.mult, ALU.add)

            k = Chain(pool, k_pool, 0)
            k(pool.memset(ident[:], 0.0))
            k(pool.affine_select(out=ident[:], in_=ident[:], compare_op=ALU.not_equal, fill=1.0, base=0,
                                 pattern=[[-1, P]], channel_multiplier=1))
            k(pool.memset(sel32[:], 0.0))
            for i in range(3):
                k(pool.affine_select(out=sel32[:], in_=sel32[:], compare_op=ALU.not_equal, fill=1.0,
                                     base=-NBC * i, pattern=[[-1, NBC]], channel_multiplier=1))
            k(pool.memset(neghalf[:], -0.5))
            k(pool.memset(econst[:], E_CONST))
            k(pool.memset(eps[:], 1e-5))
            k(pool.iota(iota8[:], pattern=[[1, E]], base=E, channel_multiplier=0, allow_small_or_imprecise_dtypes=True))

            def ln_rstd_(c, nb, start=0):
                n = slice(start, start + SB * nb)
                pool.wait_ge(ln_mv, c + 1)
                pool.tensor_tensor(veps[:, n], mv[:, n, 1], eps[:, n], ALU.add).then_inc(ln_eps, 1)
                pool.wait_ge(ln_eps, c + 1)
                pool.tensor_tensor(rstd[:, n], veps[:, n], neghalf[:, n], ALU.pow).then_inc(ln_rstd, 1)

            def rt_exp(r, nb):
                pool.wait_ge(rt_d, r + 1)
                pool.tensor_tensor(rt[0:nb, 2], econst[0:nb], rt[0:nb, 1], ALU.pow).then_inc(rt_pow, 1)

            for c in range(4):
                ln_rstd_(LN_A0 + c, 2, start=c % 2 * 2 * SB)
            k(copy(sel[:], sel32[:].unsqueeze(2).to_broadcast([PARTS, NBC, P])))

            def split_weights():
                pool.wait_ge(ld_nat, 32)
                copy(uvnat_pair[0][:], uvnat).then_inc(k_nat, 1)
                pool.wait_ge(k_nat, 1)
                pool.tensor_tensor(uvnat_pair[1][:], uvnat, uvnat_pair[0][:].bitcast(F32), ALU.subtract)\
                    .then_inc(k_natlow, 1)

            def split_stream(i):
                tok = slice(2 * i * S, (2 * i + 2) * S)
                pool.wait_ge(ln_hT, LN_F1 + i + 1)
                copy(hT_pair[0][:, tok], hT[:, tok]).then_inc(k_split, 1)
                pool.wait_ge(k_split, i + 1)
                pool.tensor_tensor(hT_pair[1][:, tok], hT[:, tok], hT_pair[0][:, tok].bitcast(F32), ALU.subtract)\
                    .then_inc(k_hTlow, 1)

            def front_parts(g):
                k_ = Chain(pool, m_partspool, 4 * g)
                pool.wait_ge(m_bcf, 2 * g + 2)
                k_(copy(parts[:, g], bcf[g][0:PARTS, :]))
                k_(pool.tensor_tensor(res[g], bcf[g][0:PARTS, :], parts[:, g], ALU.subtract))
                k_(copy(mid[2 * NBC:PARTS, :], res[g][2 * NBC:PARTS, :]))
                k_(copy(parts[NBC:2 * NBC, g], res[g][NBC:2 * NBC, :]))
                pool.tensor_tensor(parts[2 * NBC:PARTS, g], res[g][2 * NBC:PARTS, :], mid[2 * NBC:PARTS, :], ALU.subtract)\
                    .then_inc(m_parts, 1)
                pool.wait_ge(m_parts, g + 1)

            def front_poly(g):
                k_ = Chain(pool, m_polypool, 3 * g)
                pool.wait_ge(m_e, 2 * g + 2)
                k_(pool.tensor_scalar(dBu[:, 1, 0], eb[g][:, 1], 1.0 / 3.0, -0.5, ALU.mult, ALU.add))
                k_(pool.tensor_tensor(dBu[:, 1, 1], dBu[:, 1, 0], eb[g][:, 1], ALU.mult))
                k_(pool.tensor_scalar(dBu[:, 1, 0], dBu[:, 1, 1], 1.0, 1.0, ALU.mult, ALU.add))
                pool.tensor_tensor(poly[g][:, 1], dBu[:, 1, 0], eb[g][:, 1], ALU.mult).then_inc(m_poly, 1)
                pool.wait_ge(m_poly, g + 1)

            def scan_step(J, r):
                for k in range(2):
                    pool.wait_ge(s_scan[r][k], J + 1)
                    if k == 0:
                        pool.wait_ge(s_Csb[r], J + 1)
                    wait(pool, s_sum[1 - r][k], J + r)
                    pool.tensor_tensor(hC[:, k], h[:, r, k], Csb[:, r], ALU.mult).then_inc(s_hC[r][k], 1)

            split_weights()
            front_parts(0)
            for g in range(2):
                front_poly(g)
            front_parts(1)
            for g in range(2):
                J0 = g * NS // 2
                for r in range(2):
                    scan_step(J0, r)
                with pool.Fori(J0 + 1, J0 + NS // 2) as J:
                    for r in range(2):
                        scan_step(J, r)
            for g in range(2):
                ln_rstd_(LN_A1 + g, HB)
                rt_exp(RT_A + g, HB)

            for i in range(3):
                ln_rstd_(LN_F1 + i, 2)
                if i:
                    split_stream(i - 1)

            def qh_step(b, p):
                for i in range(2):
                    pool.wait_ge(a_tau[p % 2][i], cnt(pool, b, p))
                    wait(pool, a_pv[p % 2], cnt(pool, b, p - 2))
                    pool.sem_inc(pool_passed, 1)
                    pool.tensor_scalar(qh[:, p % 2, i].rearrange("p k s -> p (k s)"), tau[:, i], 0.5, 0.5,
                                       ALU.mult, ALU.add).then_inc(a_qh[p % 2][i], 1)

            def batch(b, first=False, last=False):
                prepare(pool, b)
                for p in range(NP):
                    if not (first and p == 0) and not (last and p == NP - 1):
                        qh_step(b, p + 1)
                    if not first and p == 1:
                        ln_rstd_(LN_AT - 1 + b, 1)
                    if not first and p == 5:
                        rt_exp(RT_AT - 1 + b, 1)

            qh_step(0, 0)
            ln_rstd_(LN_F1 + 3, 2)
            split_stream(2)
            qh_step(0, 1)
            split_stream(3)
            batch(0, first=True)
            with pool.Fori(1, B - 1) as b:
                batch(b)
            batch(B - 1, last=True)
            ln_rstd_(LN_AT + B - 1, 1)
            rt_exp(RT_AT + B - 1, 1)
            for i in range(3):
                pool.wait_ge(fin_x, FIN_F2 + i + 1)
                pool.dma_start(out_dram[:, 2 * i:2 * i + 2], xv[:, 2 * i:2 * i + 2]).then_inc(st_out, 16)

        @block.scalar
        def _(act):
            act.dma_start(rows[0:NIN, :], bin_.rearrange("(c p) -> c p", p=P)).then_inc(ld_rows, 16)
            act.dma_start(rows[CB_DT:CB_DT + KD, :], bdt.rearrange("(c p) -> c p", p=P)).then_inc(ld_rows, 16)
            act.dma_start(rows[CB_DP:CB_DP + KD, :], Dp.rearrange("(c p) -> c p", p=P)).then_inc(ld_rows, 16)
            act.dma_start(rows[CB_BOUT:CB_BOUT + 1, :], bout.rearrange("(c p) -> c p", p=P)).then_inc(ld_rows, 16)
            act.dma_start(rows[CB_BO:CB_BO + 1, :], bo.rearrange("(c p) -> c p", p=P)).then_inc(ld_rows, 16)
            act.dma_start(rows[CB_BP1:CB_BP1 + 1, :], bp1.rearrange("(c p) -> c p", p=P)).then_inc(ld_rows, 16)
            act.dma_start(b12rows[:, 0:FH], b1).then_inc(ld_rows, 16)
            act.dma_start(b12rows[:, FH:], b2).then_inc(ld_rows, 16)
            act.dma_start(alog[:].rearrange("p (k n) -> p k n", k=KD), A_log.rearrange("(k p) n -> p k n", p=P))\
                .then_inc(ld_scan, 16)

            def ln_copy(c, nb, tok, src):
                act.wait_ge(ln_tp, c + 1)
                act.activation(hT[:, tok], src, ACT.Copy).then_inc(ln_hT, 1)

            def fin_copy(f, nb, src, bias, scale):
                wait(act, fin_xp, f)
                act.activation(gT[:, 0:nb * S], src, ACT.Identity, bias=bias, scale=scale).then_inc(fin_gT, 1)

            def rt_gelu(r, nb, src):
                act.wait_ge(rt_r1, r + 1)
                act.activation(g1[:, 0:nb], src, ACT.Gelu, bias=cols[:, CB_BP1:CB_BP1 + 1]).then_inc(rt_g, 1)

            act.preload_act_table_set("silu_and_others")
            for c in range(2):
                ln_copy(LN_A0 + c, 2, slice(2 * c * S, 2 * (c + 1) * S), bank(c))
            act.wait_ge(k_rows, 1)
            act.copy(cols[:], bank(7, ROWS)).then_inc(k_cols, 1)
            act.wait_ge(k_b12, 1)
            act.copy(b12all[:].rearrange("p e c -> p c e"), bank(6, 3 * E).rearrange("p (c e) -> p c e", e=E))\
                .then_inc(k_b12c, 1)
            act.wait_ge(k_cols, 1)

            def scan_step(g, J, r, j, first=False):
                for k in range(2):
                    if first:
                        act.wait_ge(m_u, 4)
                    wait(act, s_scan[1 - r][k], J + r)
                    n = k * NS + r + 2 * j
                    act.activation(dA[:, k, :, 1:], delta[:, g, k].rearrange("p (b s) -> p b s", s=S)[:, :, 1:],
                                   ACT.Exp, scale=negA[:, at(n, 1, 1)]).then_inc(s_dA[r][k], 1)
                act.wait_ge(s_C[r], J + 1)
                wait(act, s_hC[r][1], J)
                act.copy(Csb[:, r], ps[:, 2 * 512:2 * 512 + HT]).then_inc(s_Csb[r], 1)

            def tail_first(g):
                act.wait_ge(fin_g, FIN_A + g + 1)
                fin_copy(FIN_A + g, HB, ps[:, 4 * 512:4 * 512 + HT], cols[:, CB_BOUT:CB_BOUT + 1], 1.0)

            def silus(g, ts):
                for t in ts:
                    mc, nb = (t % 2) + 2 * (t // 4), (t // 2) % 2
                    dst = (xs if mc < KD else zs)[:, g, mc % KD, nb * 512:(nb + 1) * 512]
                    act.wait_ge(m_inp, block_number(g, t) + 1)
                    act.activation(dst, bank(4 * g + t % 4), ACT.Silu, bias=cols[:, CB_BIN + mc:CB_BIN + mc + 1])\
                        .then_inc(m_silu, 1)

            silus(0, range(2))
            for c in range(2, 4):
                ln_copy(LN_A0 + c, 2, slice(2 * c * S, 2 * (c + 1) * S), bank(c + 2))
            silus(0, range(2, 4))
            silus(1, range(4))
            act.preload_act_table_set("natural_log_exp_and_others")
            act.wait_ge(ld_scan, 16)
            act.activation(negA[:], alog[:], ACT.Exp).then_inc(k_expA, 1)
            for g in range(2):
                for k in range(KD):
                    dt = ps[:, (4 * g + 2 * k) * 512:(4 * g + 2 * k + 2) * 512]
                    act.wait_ge(m_dt, 2 * g + k + 1)
                    act.activation(eb[g][:, k], dt, ACT.Abs, bias=cols[:, CB_DT + k:CB_DT + k + 1]).then_inc(m_abs, 1)
                    act.activation(delta[:, g, k], dt, ACT.Relu, bias=cols[:, CB_DT + k:CB_DT + k + 1]).then_inc(m_rel, 1)
                    act.wait_ge(m_abs, 2 * g + k + 1)
                    act.activation(eb[g][:, k], eb[g][:, k], ACT.Exp, scale=-1.0).then_inc(m_e, 1)
                    act.wait_ge(m_e, 2 * g + k + 1)
                    if k == 0:
                        act.activation(poly[g][:, 0], eb[g][:, 0], ACT.Copy, scale=1.0 / 3.0, bias=-0.5).then_inc(m_w, 1)
                    act.activation(lnb[g][:, k], eb[g][:, k], ACT.Ln, bias=1.0).then_inc(m_ln, 1)
            for g in range(2):
                silus(g, range(4, 8))
            act.preload_act_table_set("natural_log_exp_and_others")
            for g in range(2):
                J0 = g * NS // 2
                for r in range(2):
                    scan_step(g, J0, r, 0, first=True)
                if g:
                    tail_first(0)
                with act.Fori(1, NS // 2) as j:
                    for r in range(2):
                        scan_step(g, j + J0, r, j)
            act.preload_act_table_set("gelu_and_others")
            tail_first(1)
            ln_copy(LN_A1, HB, slice(0, HT), ps[:, 0:HT])
            rt_gelu(RT_A, HB, bank(4, HB))
            for i in range(8):
                low, w, c = i // 4, i // 2 % 2, i % 2
                act.wait_ge(k_uvf, i + 1)
                act.copy(uvfT[low][:, w, c * 512:(c + 1) * 512], bank(i % 4)).then_inc(k_uvfT, 1)
            ln_copy(LN_A1 + 1, HB, slice(HT, 2 * HT), ps[:, 4 * 512:4 * 512 + HT])

            def ffn_gelu(f, i, which=(0, 1)):
                j = 4 * f + i
                for s in which:
                    wait(act, f_r, 2 * j - 1 + s)
                    act.wait_ge(f_h, 2 * j + s + 1)
                    for c in range(2):
                        ins = act.activation(gf[:, s, c], bank(s, S, c * S), ACT.Gelu,
                                             bias=b12s[:, at(2 * i + s, 1, 1), c])
                    ins.then_inc(f_g, 1)

            def ffn_fin(f, fi):
                act.wait_ge(fin_g, fi - (B if f else 0) + 1)
                fin_copy(fi, 2, bank(3), bo3[:, 0:1], 0.3)

            def ffn(f, first_fin):
                for i in range(4):
                    if f == 0 and i >= 2:
                        ln_copy(LN_F1 + i - 2, 2, slice((2 * i - 4) * S, (2 * i - 2) * S), bank(7))
                    if i < 3:
                        ffn_gelu(f, i + 1, (0,))
                    if f == 1 and i == 0:
                        ln_copy(LN_AT + B - 1, 1, slice((B - 1) * S, B * S), bank(6, S))
                    if i < 3:
                        ffn_gelu(f, i + 1, (1,))
                    if f == 1 and i == 0:
                        rt_gelu(RT_AT + B - 1, 1, bank(6, 1))
                    ffn_fin(f, first_fin + i)

            ffn_gelu(0, 0, (0,))
            rt_gelu(RT_A + 1, HB, bank(6, HB))
            ffn_gelu(0, 0, (1,))
            ffn(0, FIN_F1)

            def tanh_step(b, p):
                for i in range(2):
                    act.wait_ge(a_f[p % 2], cnt(act, b, p))
                    wait(act, a_qh[(p - 1) % 2][i], cnt(act, b, p - 1))
                    act.activation(tau[:, i], bank(i), ACT.Tanh, scale=0.5).then_inc(a_tau[p % 2][i], 1)

            def uvT_step(b, p):
                act.wait_ge(a_uv[p % 2], cnt(act, b, p))
                wait(act, a_nt[p % 2], cnt(act, b, p - 2))
                act.mul(uvT[:, p % 2], bank(5), SCALE).then_inc(a_uvT[p % 2], 1)

            def nat_step(b, p):
                act.wait_ge(a_nt[p % 2], cnt(act, b, p))
                wait(act, a_pv[p % 2], cnt(act, b, p - 2))
                act.copy(nat[:, p % 2].rearrange("p a c -> p (a c)"), bank(6)).then_inc(a_nat[p % 2], 1)

            def batch(b, first=False, last=False):
                prepare(act, b)
                for p in range(NP):
                    if not (last and p == NP - 1):
                        tanh_step(b, p + 1)
                    wait(act, a_pv[(p - 1) % 2], cnt(act, b, p - 1))
                    act.wait_ge(a_t[p % 2][1], cnt(act, b, p))
                    act.copy(qhT[:, 1].rearrange("p k s -> p (k s)"), bank(3)).then_inc(a_qhT[p % 2][1], 1)
                    if not (last and p >= NP - 2):
                        uvT_step(b, p + 2)
                    if not first:
                        if p == 3:
                            ln_copy(LN_AT - 1 + b, 1, prev_batch(b), bank(6, S))
                        if p == 4:
                            rt_gelu(RT_AT - 1 + b, 1, bank(6, 1))
                    if first and p == 0:
                        ln_copy(LN_F1 + 3, 2, slice(6 * S, 8 * S), bank(7))
                    if not (last and p == NP - 1):
                        nat_step(b, p + 1)
                    if not first and p == 0:
                        act.wait_ge(a_g[1], cnt(act, b, -1))
                        fin_copy(FIN_AT - 1 + b, 1, bank(7, S), 0.0, SCALE)

            uvT_step(0, 0)
            tanh_step(0, 0)
            uvT_step(0, 1)
            nat_step(0, 0)
            ln_copy(LN_F1 + 2, 2, slice(4 * S, 6 * S), bank(7))
            batch(0, first=True)
            with act.Fori(1, B - 1) as b:
                batch(b)
            batch(B - 1, last=True)
            ffn_gelu(1, 0)
            act.wait_ge(a_g[1], cnt(act, B, -1))
            fin_copy(FIN_AT + B - 1, 1, bank(7, S), 0.0, SCALE)
            ffn(1, FIN_F2)

        @block.tensor
        def _(pe):
            def turn(dst, src, n=P):
                return pe.transpose(dst, src, ident[0:n, 0:n])

            def ln_turn(c, nb, dst, start=0):
                pe.wait_ge(ln_h, c + 1)
                for i in range(SB * nb):
                    ins = turn(dst[:, i * P:(i + 1) * P], hs[:, (start + i) * P:(start + i + 1) * P])
                ins.then_inc(ln_tp, 1)

            def fin_turn(f, nb, dst):
                pe.wait_ge(fin_gT, f + 1)
                for i in range(SB * nb):
                    ins = turn(dst[:, i * P:(i + 1) * P], gT[:, i * P:(i + 1) * P])
                ins.then_inc(fin_xp, 1)

            def rt_first(c, r, nb, b, dst):
                pe.wait_ge(ln_hT, c + 1)
                last = hTv[:, at(b, 1, nb), S - 1]
                pe.matmul(dst[:, 0:nb], wp1[:], last, start=True, stop=True).then_inc(rt_r1, 1)

            def rt_second(r, nb, dst):
                pe.wait_ge(rt_g, r + 1)
                pe.matmul(dst[0:nb, 64:64 + E], g1[:, 0:nb], wp2[:], start=True, stop=True).then_inc(rt_r2, 1)

            pe.wait_ge(k_pool, 2)
            for c in range(2):
                ln_turn(LN_A0 + c, 2, bank(c), start=c % 2 * 2 * SB)
            pe.wait_ge(ld_rows, 16 * 13)
            turn(bank(7, ROWS), rows[:], ROWS).then_inc(k_rows, 1)
            for c in range(3):
                ins = turn(bank(6, E, c * E), b12rows[:, c * P:(c + 1) * P], E)
            ins.then_inc(k_b12, 1)
            pe.wait_ge(ld_win, 16)

            def bcast(g, J, r, j, which):
                if which == 0:
                    wait(pe, s_uB[1 - r][1], J + r)
                else:
                    wait(pe, s_Csb[1 - r], J + r)
                row = which * NS + r + 2 * j
                for nb in range(NBK):
                    ins = pe.matmul(bank(2 * which + nb), sel[:, at(row, 1, 1), :].rearrange("q a m -> q (a m)"),
                                    parts[:, g, nb * 512:(nb + 1) * 512], start=True, stop=True)
                ins.then_inc((s_B if which == 0 else s_C)[r], 1)

            def add_up(J, r, k, stop=False):
                pe.wait_ge(s_hC[r][k], J + 1)
                for nb in range(NBK):
                    ins = pe.matmul(bank(4 + 2 * k + nb), ident[:], hC[:, k, nb * 512:(nb + 1) * 512],
                                    start=False, stop=stop)
                ins.then_inc(s_sum[r][k], 1)

            def in_projection(g, t):
                mc, nb = (t % 2) + 2 * (t // 4), (t // 2) % 2
                pe.matmul(bank(4 * g + t % 4), win[:, mc * P:(mc + 1) * P], hT[:, g * HT + nb * 512:g * HT + (nb + 1) * 512],
                          start=True, stop=True).then_inc(m_inp, 1)

            def x_projection(g, nb):
                pe.wait_ge(m_silu, 4 * g + 2 * nb + 2)
                for k in range(KD):
                    ins = pe.matmul(bank(4 * g + nb)[0:PARTS + RK, :], wx[:, k, :], xs[:, g, k, nb * 512:(nb + 1) * 512],
                                    start=(k == 0), stop=(k == KD - 1))
                ins.then_inc(m_xp, 1)

            def dt_projection(g):
                pe.wait_ge(m_silu, 4 * g + 4)
                pe.wait_ge(m_bcf, 2 * g + NBK)
                for k in range(KD):
                    for nb in range(NBK):
                        ins = pe.matmul(bank(4 * g + 2 * k + nb), wdt[PARTS:PARTS + RK, k * P:(k + 1) * P],
                                        bcf[g][PARTS:PARTS + RK, nb * 512:(nb + 1) * 512], start=True, stop=True)
                    ins.then_inc(m_dt, 1)

            def rows_of(g, r):
                for which in range(2):
                    bcast(g, g * NS // 2, r, 0, which)

            def skip_term(g, channels=range(KD)):
                for k in channels:
                    if g:
                        pe.wait_ge(*((fin_gT, FIN_A + 1) if k == 0 else (fin_x, FIN_A + 1)))
                    for nb in range(NBK):
                        pe.matmul(bank(4 + 2 * k + nb), diagD[:, k, :], xs[:, g, k, nb * 512:(nb + 1) * 512],
                                  start=True, stop=False)

            def states(g):
                J0 = g * NS // 2
                add_up(J0, 0, 0)
                with pe.Fori(1, NS // 2) as j:
                    J = pe.snap(j + J0)
                    for which in range(2):
                        bcast(g, J, 0, j, which)
                    add_up(J - 1, 0, 1)
                    add_up(J - 1, 1, 0)
                    for which in range(2):
                        bcast(g, J, 1, j, which)
                    add_up(J - 1, 1, 1)
                    add_up(J, 0, 0)

            def out_projection(g):
                pe.wait_ge(ld_late, 16 * 5)
                for k in range(KD):
                    pe.wait_ge(m_y, 2 * g + k + 1)
                    for nb in range(NBK):
                        ins = pe.matmul(bank(4 + nb), wout[:, k, :], yT[:, k, nb * 512:(nb + 1) * 512],
                                        start=(k == 0), stop=(k == KD - 1))
                ins.then_inc(fin_g, 1)

            pe.wait_ge(ln_hT, LN_A0 + 2)
            for t in range(2):
                in_projection(0, t)
            for c in range(2, 4):
                ln_turn(LN_A0 + c, 2, bank(c + 2), start=c % 2 * 2 * SB)
            for t in range(2, 4):
                in_projection(0, t)
            pe.wait_ge(ld_mamba, 16 * 5)
            for nb in range(NBK):
                x_projection(0, nb)
            pe.wait_ge(ln_hT, LN_A0 + 4)
            pe.wait_ge(k_b12c, 1)
            for t in range(4):
                in_projection(1, t)
            dt_projection(0)
            for nb in range(NBK):
                x_projection(1, nb)
            dt_projection(1)
            for g in range(2):
                pe.wait_ge(m_rel, 2 * g + 2)
                for t in range(4, 8):
                    in_projection(g, t)
            pe.wait_ge(m_parts, 1)
            pe.wait_ge(k_pool, 11)
            pe.wait_ge(m_silu, 12)
            rows_of(0, 0)
            pe.wait_ge(m_silu, 16)
            pe.wait_ge(k_dve, 2)
            skip_term(0, (0,))
            rows_of(0, 1)
            skip_term(0, (1,))
            states(0)
            last = NS // 2 - 1
            pe.wait_ge(m_parts, 2)
            rows_of(1, 0)
            add_up(last, 0, 1)
            for k in range(KD):
                add_up(last, 1, k, stop=True)
            rows_of(1, 1)
            out_projection(0)
            fin_turn(FIN_A, HB, ps[:, 6 * 512:6 * 512 + HT])
            skip_term(1)
            states(1)
            add_up(NS // 2 + last, 0, 1)
            for k in range(KD):
                add_up(NS // 2 + last, 1, k, stop=True)
            out_projection(1)
            ln_turn(LN_A1, HB, ps[:, 0:HT])
            fin_turn(FIN_A + 1, HB, ps[:, 6 * 512:6 * 512 + HT])
            rt_first(LN_A1, RT_A, HB, 0, bank(4))
            pe.wait_ge(k_natlow, 1)
            for i in range(8):
                low, w, c = i // 4, i // 2 % 2, i % 2
                if low:
                    pe.wait_ge(k_uvfT, i - 3)
                for n in range(4):
                    ins = turn(bank(i % 4, P, n * P), uvnat_pair[low][:, w, 4 * c + n, :].bitcast(F32))
                ins.then_inc(k_uvf, 1)
                if i == 2:
                    rt_second(RT_A, HB, bank(4))

            def rt_turn(g):
                pe.wait_ge(rt_row, g + 1)
                turn(bank(6, HB, P)[0:1, :], rs[0:HB, 4:5], HB).then_inc(rt_turned, 1)

            rt_turn(0)
            ln_turn(LN_A1 + 1, HB, ps[:, 4 * 512:4 * 512 + HT])
            pe.wait_ge(k_uvfT, 8)

            def ffn_hidden(f, i, which=(0, 1)):
                j = 4 * f + i
                for s in which:
                    slot = 2 * (j % 2) + s
                    pe.wait_ge(w1_ld[slot], 32 * (j // 2) + 32)
                    wait(pe, f_g, 2 * j - 1 + s)
                    for c in range(2):
                        ins = pe.matmul(bank(s, S, c * S), w1s[:, slot, c * P:(c + 1) * P],
                                        hT[:, (2 * i + s) * S:(2 * i + s + 1) * S], start=True, stop=True)
                    ins.then_inc(f_h, 1)

            def ffn_second(f, i, which=(0, 1)):
                j = 4 * f + i
                for s in which:
                    slot = 2 * (j % 2) + s
                    pe.wait_ge(w2_ld[slot], 16 * (j // 2) + 16)
                    wait(pe, f_rT, 2 * j - 1 + s)
                    pe.wait_ge(f_g, 2 * j + s + 1)
                    for c in range(2):
                        ins = pe.matmul(bank(2 + 3 * s, S), w2s[:, slot, c, :], gf[:, s, c], start=(c == 0), stop=(c == 1))
                    ins.then_inc(f_r, 1)

            def ffn_out(f, i):
                pe.wait_ge(f_rT, 2 * (4 * f + i) + 2)
                wait(pe, fin_gT, (FIN_F1 if f == 0 else FIN_F2) + i)
                pe.matmul(bank(3), wo[:], rT[:], start=True, stop=True).then_inc(fin_g, 1)

            def ffn(f, first_fin):
                for i in range(4):
                    ffn_second(f, i, (0,))
                    if f == 1 and i == 1:
                        rt_second(RT_AT + B - 1, 1, bank(6))
                    ffn_second(f, i, (1,))
                    if i:
                        if i > 1:
                            pe.wait_ge(fin_x, first_fin + i - 1)
                        fin_turn(first_fin + i - 1, 2, bank(4))
                    if f == 0 and i >= 2:
                        ln_turn(LN_F1 + i - 2, 2, bank(7))
                    if i < 3:
                        ffn_hidden(f, i + 1)
                    if f == 1 and i == 0:
                        pe.wait_ge(fin_x, FIN_AT + B)
                        ln_turn(LN_AT + B - 1, 1, bank(6, S))
                    ffn_out(f, i)
                    if f == 0 and i == 0:
                        rt_turn(1)
                    if f == 1 and i == 0:
                        rt_first(LN_AT + B - 1, RT_AT + B - 1, 1, B - 1, bank(6))

            ffn_hidden(0, 0, (0,))
            rt_first(LN_A1 + 1, RT_A + 1, HB, HB, bank(6))
            ffn_hidden(0, 0, (1,))
            rt_second(RT_A + 1, HB, bank(6))
            ffn(0, FIN_F1)

            PARTS_OF_PRODUCT = ((0, 0), (0, 1), (1, 0))

            def split_matmul(dst, stationary, moving, start=True, stop=True):
                for n, (i, j) in enumerate(PARTS_OF_PRODUCT):
                    ins = pe.matmul(dst, stationary[i], moving[j], start=start and n == 0, stop=stop and n == 2)
                return ins

            def project(b, p):
                off = p // NP
                tok = bass.ds(b * S + off * S, S) if runtime(b) else slice((b + off) * S, (b + off + 1) * S)
                cols_p = slice((p % NP) * P, (p % NP + 1) * P)
                wait(pe, a_uvT[(p - 1) % 2], cnt(pe, b, p - 1))
                for w in range(2):
                    ins = split_matmul(bank(5, S, w * S), [a[:, w, cols_p] for a in uvfT],
                                       [a[:, tok] for a in hT_pair])
                ins.then_inc(a_pr[p % 2], 1)

            def messages(b, p):
                pe.wait_ge(a_uv[p % 2], cnt(pe, b, p))
                wait(pe, a_tau[(p - 1) % 2][1], cnt(pe, b, p - 1))
                for k in range(SB):
                    for n, (a, c) in enumerate(PARTS_OF_PRODUCT):
                        for i in range(2):
                            head = slice(i * R, (i + 1) * R)
                            ins = pe.matmul(bank(i, S, k * S), uvT_pair[a][head, p % 2, k * P:(k + 1) * P],
                                            uvT_pair[c][head, p % 2, S:2 * S], start=(n == 0), stop=(n == 2))
                ins.then_inc(a_f[p % 2], 1)

            def turn_uv(b, p):
                pe.wait_ge(a_uvT[p % 2], cnt(pe, b, p))
                wait(pe, a_nat[(p - 1) % 2], cnt(pe, b, p - 1))
                for i in range(4):
                    ins = turn(bank(6, P, i * P), uvT[:, p % 2, i * P:(i + 1) * P])
                ins.then_inc(a_nt[p % 2], 1)

            def turn_qh(b, p):
                for i in range(2):
                    wait(pe, a_qhT[(p - 1) % 2][i], cnt(pe, b, p - 1))
                    pe.wait_ge(a_qh[p % 2][i], cnt(pe, b, p))
                    for k in range(SB):
                        for t in range(SB):
                            ins = turn(bank(2 + i, P, t * S + k * P), qh[:, p % 2, i, k, t * P:(t + 1) * P])
                    ins.then_inc(a_t[p % 2][i], 1)

            def qhT_u(b, p):
                pe.wait_ge(a_nat[p % 2], cnt(pe, b, p))
                wait(pe, a_v12[(p - 1) % 2], cnt(pe, b, p - 1))
                for k in range(SB):
                    for i in range(2):
                        pe.matmul(ps[i * R:(i + 1) * R, 4 * 512 + S:5 * 512], nat[:, p % 2, k, i * R:(i + 1) * R],
                                  qh[:, p % 2, i, k, :], start=(k == 0), stop=(k == SB - 1))

            def qh_v(b, p):
                for i in range(2):
                    pe.wait_ge(a_qhT[p % 2][i], cnt(pe, b, p))
                for t in range(SB):
                    for i in range(2):
                        ins = pe.matmul(ps[i * R:(i + 1) * R, 4 * 512:4 * 512 + S], nat[:, p % 2, SB + t, i * R:(i + 1) * R],
                                        qhT[:, i, t, :], start=(t == 0), stop=(t == SB - 1))
                ins.then_inc(a_pv[p % 2], 1)

            def sum_pair(b, p):
                pe.wait_ge(a_v12[p % 2], cnt(pe, b, p))
                for w in range(2):
                    ins = split_matmul(bank(7, S), [a[:, w, p % NP, :] for a in uvnat_pair],
                                       [a[:, p % 2, w * S:(w + 1) * S] for a in v12T_pair],
                                       start=(p % NP == 0 and w == 0), stop=(p % NP == NP - 1 and w == 1))
                ins.then_inc(a_g[p % 2], 1)

            def batch(b, first=False, last=False):
                prepare(pe, b)
                for p in range(NP):
                    if not (last and p == NP - 1):
                        messages(b, p + 1)
                    if not (last and p >= NP - 2):
                        project(b, p + 2)
                    if not first and p in (1, 3, 4, 5):
                        pe.wait_ge(a_nat[p % 2], cnt(pe, b, p))
                        if p == 1:
                            fin_turn(FIN_AT - 1 + b, 1, bank(6, S))
                        if p == 3:
                            ln_turn(LN_AT - 1 + b, 1, bank(6, S))
                        if p == 4:
                            rt_first(LN_AT - 1 + b, RT_AT - 1 + b, 1, b - 1, bank(6))
                        if p == 5:
                            rt_second(RT_AT - 1 + b, 1, bank(6))
                    turn_qh(b, p)
                    qhT_u(b, p)
                    if first and p == 0:
                        pe.wait_ge(ln_hT, LN_F1 + 3)
                        ln_turn(LN_F1 + 3, 2, bank(7))
                    if first and p == 1:
                        pe.wait_ge(ln_hT, LN_F1 + 4)
                    if not (first and p == 0):
                        sum_pair(b, p - 1)
                    qh_v(b, p)
                    if not first:
                        if p == 1:
                            pe.wait_ge(fin_x, FIN_AT + b)
                        if p == 3:
                            pe.wait_ge(ln_hT, LN_AT + b)
                        if p == 4:
                            pe.wait_ge(rt_g, RT_AT + b)
                        if p == 5:
                            pe.wait_ge(rt_d, RT_AT + b)
                    if not (last and p == NP - 1):
                        turn_uv(b, p + 1)

            pe.wait_ge(fin_x, FIN_F1 + 3)
            fin_turn(FIN_F1 + 3, 2, bank(4))
            pe.wait_ge(k_hTlow, 1)
            project(0, 0)
            messages(0, 0)
            project(0, 1)
            turn_uv(0, 0)
            ln_turn(LN_F1 + 2, 2, bank(7))
            batch(0, first=True)
            pe.wait_ge(k_hTlow, 4)
            with pe.Fori(1, B - 1) as b:
                batch(b)
            batch(B - 1, last=True)
            ffn_hidden(1, 0)
            sum_pair(B - 1, NP - 1)
            fin_turn(FIN_AT + B - 1, 1, bank(6, S))
            ffn(1, FIN_F2)
            pe.wait_ge(fin_x, FIN_F2 + 3)
            fin_turn(FIN_F2 + 3, 2, bank(4))

        @block.vector
        def _(dve):
            def ln_stats(c, nb, blk, start=0, ahead=0):
                for i in range(start, start + SB * nb):
                    ins = dve.bn_stats(stats[:, i, :], x[:, blk(i - start)])
                ins.then_inc(ln_stat, 1)
                wait(dve, ln_h, c - ahead)
                dve.wait_ge(ln_stat, c + 1)
                dve.sem_inc(dve_passed, 1)
                for i in range(start, start + SB * nb):
                    ins = dve.bn_aggr(mv[:, i, :], stats[:, i, :])
                ins.then_inc(ln_mv, 1)

            def ln_norm(c, nb, blk, xh=None, start=0, ahead=0):
                wait(dve, ln_tp, c - ahead)
                dve.wait_ge(ln_rstd, c + 1)
                for i in range(SB * nb):
                    n = start + i
                    ins = dve.tensor_scalar(hs[:, n * P:(n + 1) * P], x[:, blk(i)], mv[:, n, 0:1], rstd[:, n:n + 1],
                                            ALU.subtract, ALU.mult)
                ins.then_inc(ln_h, 1)
                if xh is not None:
                    dve.wait_ge(ln_h, c + 1)
                    whole = blk(0, SB * nb)
                    dve.tensor_tensor(x[:, whole], x[:, whole], hs[:, 0:SB * nb * P], ALU.add).then_inc(ln_xh, 1)

            def fin_add(f, nb, tok, src):
                dve.wait_ge(fin_xp, f + 1)
                dve.tensor_tensor(x[:, tok], src, x[:, tok], ALU.add).then_inc(fin_x, 1)
                dve.wait_ge(fin_x, f + 1)

            def rt_logits(r, nb, src):
                k = Chain(dve, rt_chain, r * RT_STEPS)
                dve.wait_ge(rt_r2, r + 1)
                k(dve.tensor_tensor(rt[0:nb, 0], src[0:nb, 64:64 + E], bp2r[0:nb], ALU.add))
                k(dve.tensor_reduce(rs[0:nb, 0:1], rt[0:nb, 0], AX, ALU.max))
                dve.tensor_tensor(rt[0:nb, 1], rt[0:nb, 0], rs[0:nb, 0:1].to_broadcast([nb, E]), ALU.subtract)\
                    .then_inc(rt_d, 1)

            def rt_choose(r, nb, col):
                k = Chain(dve, rt_chain, r * RT_STEPS + 2)
                dve.wait_ge(rt_pow, r + 1)
                k(dve.tensor_reduce(rs[0:nb, 1:2], rt[0:nb, 2], AX, ALU.add))
                k(dve.reciprocal(rs[0:nb, 2:3], rs[0:nb, 1:2]))
                k(dve.tensor_tensor(rt[0:nb, 3], rt[0:nb, 2], rs[0:nb, 2:3].to_broadcast([nb, E]), ALU.mult))
                k(dve.tensor_reduce(rs[0:nb, 3:4], rt[0:nb, 3], AX, ALU.max))
                k(dve.tensor_tensor(rt[0:nb, 4], rt[0:nb, 3], rs[0:nb, 3:4].to_broadcast([nb, E]), ALU.is_ge))
                k(dve.tensor_scalar(rt[0:nb, 4], rt[0:nb, 4], -float(E), None, ALU.mult))
                k(dve.tensor_tensor(rt[0:nb, 5], rt[0:nb, 4], iota8[0:nb], ALU.add))
                k(dve.tensor_reduce(rs[0:nb, 4:5], rt[0:nb, 5], AX, ALU.min))
                if nb == 1:
                    dve.tensor_copy(idx[:, col], rs[0:1, 4:5]).then_inc(rt_idx, 1)
                else:
                    dve.sem_inc(rt_row, 1)
                    dve.wait_ge(rt_turned, r + 1)
                    dve.tensor_copy(idx[:, col], bank(6, nb, P)[0:1, :]).then_inc(rt_idx, 1)

            def blocks(start, scale=1):
                def blk(i, n=1):
                    if runtime(start):
                        return bass.ds(start * P + i * P, n * P)
                    return slice((start + i) * P, (start + i + n) * P)
                return blk

            for g in range(2):
                dve.wait_ge(ld_x[g], 16)
                for c in range(2 * g, 2 * g + 2):
                    ln_stats(LN_A0 + c, 2, blocks(c * 2 * SB), start=c % 2 * 2 * SB, ahead=1)
                for c in range(2 * g, 2 * g + 2):
                    ln_norm(LN_A0 + c, 2, blocks(c * 2 * SB), start=c % 2 * 2 * SB, ahead=1)
            dve.wait_ge(k_cols, 1)
            dve.wait_ge(k_pool, 10)
            dve.tensor_scalar(bo3[:], cols[:, CB_BO:CB_BO + 1], 0.3, None, ALU.mult).then_inc(k_dve, 1)
            for k in range(KD):
                ins = dve.tensor_scalar(diagD[:, k, :], ident[:], cols[:, CB_DP + k:CB_DP + k + 1], None, ALU.mult)
            ins.then_inc(k_dve, 1)

            def scan_step(g, J, r, first=False):
                for k in range(KD):
                    if k == 0:
                        dve.wait_ge(s_B[r], J + 1)
                    wait(dve, s_scan[r][k], J)
                    dve.tensor_tensor(dBu[:, r, k], ps[:, 0:HT], u[:, g, k], ALU.mult).then_inc(s_uB[r][k], 1)
                    if k == 0:
                        if not first:
                            scan(J - 1 + r, 1 - r, 1)
                    else:
                        scan(J, r, 0)

            def scan(J, r, k):
                dve.wait_ge(s_dA[r][k], J + 1)
                dve.wait_ge(s_uB[r][k], J + 1)
                wait(dve, s_hC[r][k], J)
                dve.tensor_tensor_scan(h[:, r, k], dA[:, k].rearrange("p b s -> p (b s)"), dBu[:, r, k], 0.0,
                                       ALU.mult, ALU.add).then_inc(s_scan[r][k], 1)

            def xp_copy(g, nb):
                if g:
                    dve.wait_ge(k_natlow, 1)
                dve.wait_ge(m_xp, 2 * g + nb + 1)
                dve.tensor_scalar(bcf[g][:, nb * 512:(nb + 1) * 512], bank(4 * g + nb)[0:PARTS + RK, :],
                                  cols[0:PARTS + RK, CB_BX:CB_BX + 1], None, ALU.add).then_inc(m_bcf, 1)

            def gated(g, k):
                dve.wait_ge(s_sum[1][k], (g + 1) * NS // 2)
                dve.tensor_tensor(yT[:, k], ps[:, (4 + 2 * k) * 512:(6 + 2 * k) * 512], zs[:, g, k], ALU.mult)\
                    .then_inc(m_y, 1)

            def series(g, k, k_):
                dve.wait_ge(m_e, 2 * g + k + 1)
                e = eb[g][:, k]
                k_(dve.tensor_scalar(small[:], e, LOG1P_SPLIT, None, ALU.is_lt))
                if k == 0:
                    dve.wait_ge(m_w, g + 1)
                    k_(dve.tensor_tensor(dBu[:, 0, 1], poly[g][:, 0], e, ALU.mult))
                    k_(dve.scalar_tensor_tensor(out=poly[g][:, 0], in0=dBu[:, 0, 1], scalar=1.0, in1=e, op0=ALU.add,
                                                op1=ALU.mult))
                else:
                    dve.wait_ge(m_poly, g + 1)

            def finish_delta(g, k, k_):
                dve.wait_ge(m_ln, 2 * g + k + 1)
                k_(dve.copy_predicated(lnb[g][:, k], small[:], poly[g][:, k]))
                k_(dve.tensor_tensor(delta[:, g, k], delta[:, g, k], lnb[g][:, k], ALU.add))
                dve.tensor_tensor(u[:, g, k], delta[:, g, k], xs[:, g, k], ALU.mult).then_inc(m_u, 1)

            xp_banks = ps[:, 6 * 512:6 * 512 + HT]
            for nb in range(NBK):
                xp_copy(0, nb)
            k_ = Chain(dve, m_chain, 0)
            for g, k in ((0, 0), (1, 0), (0, 1), (1, 1)):
                if (g, k) == (0, 0):
                    for nb in range(NBK):
                        xp_copy(1, nb)
                series(g, k, k_)
                if (g, k) == (0, 0):
                    dve.wait_ge(k_expA, 1)
                    dve.tensor_scalar(negA[:], negA[:], -1.0, None, ALU.mult).then_inc(k_dve, 1)
                finish_delta(g, k, k_)
            dve.memset(dA[:, :, :, 0], 0.0).then_inc(k_dve, 1)
            dve.wait_ge(m_u, 4)
            for g in range(2):
                J0 = g * NS // 2
                scan_step(g, J0, 0, first=True)
                if g:
                    for k in range(KD):
                        gated(0, k)
                scan_step(g, J0, 1)
                if g:
                    fin_add(FIN_A, HB, slice(0, HT), xp_banks)
                    ln_stats(LN_A1, HB, blocks(0))
                with dve.Fori(J0 + 1, J0 + NS // 2) as J:
                    for r in range(2):
                        scan_step(g, J, r)
                scan(J0 + NS // 2 - 1, 1, 1)
            for k in range(KD):
                gated(1, k)
            ln_norm(LN_A1, HB, blocks(0), xh=XH_A)
            fin_add(FIN_A + 1, HB, slice(HT, 2 * HT), xp_banks)
            dve.wait_ge(ld_late, 16 * 5)
            rt_logits(RT_A, HB, bank(4))
            ln_stats(LN_A1 + 1, HB, blocks(2 * HB))
            rt_choose(RT_A, HB, slice(0, HB))
            ln_norm(LN_A1 + 1, HB, blocks(2 * HB), xh=XH_A + 1)
            rt_logits(RT_A + 1, HB, bank(6))

            def ffn_bias(f, i):
                j = 4 * f + i
                for s in range(2):
                    if s == 0:
                        wait(dve, fin_g, 2 + j)
                    dve.wait_ge(f_r, 2 * j + s + 1)
                    dve.tensor_scalar(rT[:, s * S:(s + 1) * S], bank(2 + 3 * s, S), b12s[:, at(2 * i + s, 1, 1), 2],
                                      None, ALU.add).then_inc(f_rT, 1)

            def ffn(f, first_fin):
                for i in range(4):
                    if f == 0 and i >= 2:
                        ln_norm(LN_F1 + i - 2, 2, blocks(4 * i - 8))
                    if f == 1 and i == 1:
                        rt_logits(RT_AT + B - 1, 1, bank(6))
                    ffn_bias(f, i)
                    if f == 0 and i == 0:
                        rt_choose(RT_A + 1, HB, slice(HB, B))
                    if i:
                        fin_add(first_fin + i - 1, 2, slice((2 * i - 2) * S, 2 * i * S), bank(4))
                    if f == 0 and i:
                        ln_stats(LN_F1 + i - 1, 2, blocks(4 * i - 4))
                    if f == 1 and i == 0:
                        ln_norm(LN_AT + B - 1, 1, blocks(2 * B - 2), xh=True)
                        dve.wait_ge(ln_xh, XH_AT + B)
                    if f == 1 and i == 1:
                        rt_choose(RT_AT + B - 1, 1, slice(2 * B - 1, 2 * B))

            dve.wait_ge(ln_xh, XH_A + 2)
            ffn(0, FIN_F1)

            def uv_step(b, p):
                wait(dve, a_f[p % 2], cnt(dve, b, p - 2))
                dve.wait_ge(a_pr[p % 2], cnt(dve, b, p))
                dve.tensor_scalar(uvT_pair[0][:, p % 2], bank(5), SCALE, None, ALU.mult).then_inc(a_uvh[p % 2], 1)
                dve.wait_ge(a_uvh[p % 2], cnt(dve, b, p))
                dve.scalar_tensor_tensor(out=uvT_pair[1][:, p % 2], in0=bank(5), scalar=SCALE,
                                         in1=uvT_pair[0][:, p % 2].bitcast(F32), op0=ALU.mult, op1=ALU.subtract)\
                    .then_inc(a_uv[p % 2], 1)

            def batch(b, first=False, last=False):
                prepare(dve, b)
                prev = blocks(b * 2 - 2)
                for p in range(NP):
                    if not (last and p >= NP - 2):
                        uv_step(b, p + 2)
                    if not first and p == 1:
                        fin_add(FIN_AT - 1 + b, 1, prev_batch(b), bank(6, S))
                    wait(dve, a_pv[(p - 1) % 2], cnt(dve, b, p - 1))
                    dve.wait_ge(a_t[p % 2][0], cnt(dve, b, p))
                    dve.tensor_copy(qhT[:, 0].rearrange("p k s -> p (k s)"), bank(2)).then_inc(a_qhT[p % 2][0], 1)
                    if not first:
                        if p == 1:
                            ln_stats(LN_AT - 1 + b, 1, prev)
                        if p == 2:
                            ln_norm(LN_AT - 1 + b, 1, prev, xh=True)
                        if p == 5:
                            rt_logits(RT_AT - 1 + b, 1, bank(6))
                        if p == 6:
                            rt_choose(RT_AT - 1 + b, 1, bass.ds(b + (B - 1), 1) if runtime(b) else slice(B + b - 1, B + b))
                    wait(dve, a_g[p % 2], cnt(dve, b, p - 2))
                    dve.wait_ge(a_pv[p % 2], cnt(dve, b, p))
                    dve.tensor_copy(v12T_pair[0][:, p % 2], bank(4)).then_inc(a_v12h[p % 2], 1)
                    dve.wait_ge(a_v12h[p % 2], cnt(dve, b, p))
                    dve.tensor_tensor(v12T_pair[1][:, p % 2], bank(4), v12T_pair[0][:, p % 2].bitcast(F32), ALU.subtract)\
                        .then_inc(a_v12[p % 2], 1)

            uv_step(0, 0)
            ln_norm(LN_F1 + 2, 2, blocks(8))
            fin_add(FIN_F1 + 3, 2, slice(6 * S, 8 * S), bank(4))
            uv_step(0, 1)
            ln_stats(LN_F1 + 3, 2, blocks(12))
            ln_norm(LN_F1 + 3, 2, blocks(12))
            batch(0, first=True)
            with dve.Fori(1, B - 1) as b:
                batch(b)
            batch(B - 1, last=True)
            fin_add(FIN_AT + B - 1, 1, slice((B - 1) * S, B * S), bank(6, S))
            ln_stats(LN_AT + B - 1, 1, blocks(2 * B - 2))
            ffn(1, FIN_F2)
            fin_add(FIN_F2 + 3, 2, slice(6 * S, 8 * S), bank(4))


_INS = ['L0_attn_a_x', 'L0_attn_a_Win', 'L0_attn_a_bin', 'L0_attn_a_Wx', 'L0_attn_a_bx', 'L0_attn_a_Wdt',
        'L0_attn_a_bdt', 'L0_attn_a_A_log', 'L0_attn_a_Dp', 'L0_attn_a_Wout', 'L0_attn_a_bout',
        'L0_attn_b_ternary_factor_u', 'L0_attn_b_ternary_factor_v', 'L0_ffn_Wp1', 'L0_ffn_bp1', 'L0_ffn_Wp2',
        'L0_ffn_bp2', 'L0_ffn_W1', 'L0_ffn_b1', 'L0_ffn_W2', 'L0_ffn_b2', 'L0_ffn_Wo', 'L0_ffn_bo']


def kernel(**inputs):
    import numpy as np
    import concourse.bacc as bacc
    from concourse.bass_utils import run_bass_kernel_spmd

    nc = bacc.Bacc("TRN2", target_bir_lowering=False, num_devices=1)
    arrays, args = {}, []
    for name in _INS:
        a = np.ascontiguousarray(inputs[name])
        arrays[f"in_{name}"] = a
        args.append(nc.dram_tensor(f"in_{name}", a.shape, mybir.dt.from_np(a.dtype), kind="ExternalInput").ap())
    out = nc.dram_tensor("out_x", inputs['L0_attn_a_x'].shape, F32, kind="ExternalOutput").ap()
    build(nc, *args, out)
    result = run_bass_kernel_spmd(nc, [arrays], core_ids=[0])
    return result.results[0]["out_x"]
```
